# Optimizing a Trainium2 kernel written in Bass

```python
import numpy as np
import jax
import jax.numpy as jnp

def _softmax(x, axis=-1):
    return jax.nn.softmax(x, axis=axis)

def _gelu(x):
    return jax.nn.gelu(x, approximate=True)

def _silu(x):
    return jax.nn.silu(x)

def _sigmoid(x):
    return jax.nn.sigmoid(x)

def _layernorm(x, axis=-1, eps=1e-05):
    m = jnp.mean(x, axis=axis, keepdims=True)
    v = jnp.var(x, axis=axis, keepdims=True)
    return (x - m) / jnp.sqrt(v + eps)

def _scatter_add(tgt, idx, src, axis=0):
    return tgt.at[idx].add(src)

def _segment_sum(src, seg, n):
    return jax.ops.segment_sum(src, seg, n)
kernel_name = 'mk_gnn_resnorm_d1_gnn_r32_36da2e'

def setup_inputs(seed: int=0):
    np.random.seed(seed)
    _w = jnp.asarray

    def _rec_inputs():
        import jax
        import jax.numpy as jnp
        _gk = jax.random.key(seed)
        x = -8.776e-05 + 1 * jax.random.normal(jax.random.fold_in(_gk, 1), (3125, 256), jnp.float32)
        src = jax.random.randint(jax.random.fold_in(_gk, 2), (50000,), 0, 3125, jnp.int32)
        dst = jax.random.randint(jax.random.fold_in(_gk, 3), (50000,), 0, 3125, jnp.int32)
        _o = jnp.argsort(dst, stable=True)
        src = src[_o]
        dst = dst[_o]
        edge_type_8 = jax.random.randint(jax.random.fold_in(_gk, 12), (50000,), 0, 8, jnp.int32)
        return (x, src, dst, edge_type_8)
    x, src, dst, edge_type_8 = _rec_inputs()

    def _L0_gnn_setup():
        import jax, jax.numpy as jnp
        import numpy as np
        N_NODES = 625
        N_EDGES = 10000
        NUM_RELS = 8
        DIM = 256
        BN_EPS = 1e-05
        key = jax.random.key(seed)
        k1, k2, k3, k4, k5 = jax.random.split(key, 5)
        h = jax.random.normal(k1, (N_NODES, DIM), dtype=jnp.float32)
        weight = jax.random.normal(k2, (NUM_RELS, DIM, DIM), dtype=jnp.float32) * 0.05
        gamma = jnp.ones((DIM,), dtype=jnp.float32)
        beta = jnp.zeros((DIM,), dtype=jnp.float32)
        src = jax.random.randint(k3, (N_EDGES,), 0, N_NODES, dtype=jnp.int32)
        dst = jax.random.randint(k4, (N_EDGES,), 0, N_NODES, dtype=jnp.int32)
        rel = jax.random.randint(k5, (N_EDGES,), 0, NUM_RELS, dtype=jnp.int32)
        return {'h': h, 'weight': weight, 'gamma': gamma, 'beta': beta, 'src': src, 'dst': dst, 'rel': rel}
    _L0_gnn_all = _L0_gnn_setup()
    _L0_gnn_in = {k: v for k, v in _L0_gnn_all.items() if k in ('weight', 'gamma', 'beta')}
    del _L0_gnn_all
    return {'x': x, 'src': src, 'dst': dst, 'edge_type_8': edge_type_8, 'L0_gnn_weight': _L0_gnn_in['weight'], 'L0_gnn_gamma': _L0_gnn_in['gamma'], 'L0_gnn_beta': _L0_gnn_in['beta']}

def reference(x, src, dst, edge_type_8, L0_gnn_weight, L0_gnn_gamma, L0_gnn_beta):
    import jax
    import jax.numpy as jnp

    def _L0_gnn_ref(h, weight, gamma, beta, src, dst, rel):
        import jax, jax.numpy as jnp
        import numpy as np
        N_NODES = 625
        N_EDGES = 10000
        NUM_RELS = 8
        DIM = 256
        BN_EPS = 1e-05
        all_h = jnp.einsum('ni,rio->nro', h, weight)
        msg = all_h[src, rel]
        agg = jax.ops.segment_sum(msg, dst, num_segments=h.shape[0])
        mean = jnp.mean(agg, axis=0)
        var = jnp.mean(jnp.square(agg - mean), axis=0)
        out = (agg - mean) * jax.lax.rsqrt(var + BN_EPS) * gamma + beta
        return out
    x = _layernorm(x + _L0_gnn_ref(x, L0_gnn_weight, L0_gnn_gamma, L0_gnn_beta, src, dst, edge_type_8), axis=-1)
    return x

_drawn_inputs = setup_inputs


def setup_inputs(seed=0):
    import zlib

    import numpy as np

    out = dict(_drawn_inputs(seed))
    spreads = {'L0_gnn_gamma': (1.0, 0.2), 'L0_gnn_beta': (0.0, 0.1)}
    factors = {}
    for name, (base, spread) in spreads.items():
        noise = np.random.default_rng([zlib.crc32(name.encode()), seed]).standard_normal(out[name].shape)
        drawn = base * np.exp(spread * noise) if base else spread * noise
        out[name] = jnp.asarray(drawn.astype(out[name].dtype))
    for name, factor in factors.items():
        out[name] = (out[name] * factor).astype(out[name].dtype)
    return out
```

```python
from contextlib import ExitStack

import concourse.bass as bass
from concourse import mybir

F32 = mybir.dt.float32
I32 = mybir.dt.int32
ALU = mybir.AluOpType
ACT = mybir.ActivationFunctionType
AX = mybir.AxisListType

P = 128
NODES, DIM, RELS, EDGES = 3125, 256, 8, 50000
EPS = 1e-5
HALVES = DIM // P
CHUNKS = -(-EDGES // P)
LAST_EDGES = EDGES - (CHUNKS - 1) * P
TILES = -(-NODES // P)
LAST_NODES = NODES - (TILES - 1) * P
WINDOW = P // RELS
PHASE = 16
PHASES = CHUNKS // PHASE
REST = CHUNKS - PHASES * PHASE
HALF = PHASE // 2
PROJECT_AT = HALF
REST_PROJECT_AT = 4
RING_TILES = 4
RING = RING_TILES * P
REL_STRIDE = 4096
FULL_BLOCKS = CHUNKS // P
REST_CHUNKS = CHUNKS - FULL_BLOCKS * P
BLOCKS = FULL_BLOCKS + 1
TABLE = BLOCKS * P
PAD_TILES = 2
SEL_SLOTS, SUM_SLOTS = 4, 4
LOOKAHEAD = 2
GROUP = 5
GROUPS = TILES // GROUP
ROW_SLOTS = 4


def build(nc, x, src, dst, rel, weight, gamma, beta, out):
    with ExitStack() as ctx:
        def sb(name, shape, dt=F32):
            return ctx.enter_context(nc.sbuf_tensor(name, shape, dt))

        def sem(name):
            return ctx.enter_context(nc.semaphore(name))

        src_rows = sb("src_rows", [P, BLOCKS, P], I32)
        dst_rows = sb("dst_rows", [P, BLOCKS, P], I32)
        rel_rows = sb("rel_rows", [P, BLOCKS, P], I32)
        src_f = sb("src_f", [P, BLOCKS, P])
        base = sb("base", [P, BLOCKS])
        offset = sb("offset", [P, BLOCKS, P])
        key_rows = sb("key_rows", [P, BLOCKS, P])
        extremes = sb("extremes", [P, 2, BLOCKS])
        chunk_no = sb("chunk_no", [P, 4, BLOCKS], I32)
        bounds = sb("bounds", [P, 2, BLOCKS])
        broken = sb("broken", [P, 4, BLOCKS])
        violations = sb("violations", [1, 1], I32)
        source = sb("source", [P, TABLE], I32)
        key = sb("key", [P, TABLE])
        place = sb("place", [1, TABLE], I32)
        staged = sb("staged", [P, 2, HALF], I32)
        rows = sb("rows", [P, PHASE, DIM])
        lattice = sb("lattice", [P, RELS, WINDOW])
        lattice_tile = sb("lattice_tile", [P, RELS, P])
        select = sb("select", [P, SEL_SLOTS, RELS, WINDOW])
        select_tile = sb("select_tile", [P, RELS, P])
        ident = sb("ident", [P, P])
        ones = sb("ones", [P, P])
        zeros = sb("zeros", [P, P])
        ring = sb("ring", [P, HALVES, RELS, RING + WINDOW])
        w_sb = sb("w_sb", [P, RELS, HALVES, DIM])
        agg_t = sb("agg_t", [P, HALVES, (PAD_TILES + TILES) * P])
        stats = sb("stats", [P, HALVES, PAD_TILES + TILES, 6])
        bn = sb("bn", [P, HALVES, 2])
        bn_sd = sb("bn_sd", [P, HALVES])
        bn_rs = sb("bn_rs", [P, HALVES])
        bn_scale = sb("bn_scale", [P, HALVES])
        bn_shift = sb("bn_shift", [P, HALVES])
        gamma_t = sb("gamma_t", [P, HALVES])
        beta_t = sb("beta_t", [P, HALVES])
        eps = sb("eps", [P, 1])
        z = sb("z", [P, TILES, DIM])
        ln_stats = sb("ln_stats", [P, TILES, 6])
        ln = sb("ln", [P, TILES, 2])
        ln_sd = sb("ln_sd", [P, TILES])
        ln_rs = sb("ln_rs", [P, TILES])
        ln_shift = sb("ln_shift", [P, TILES])

        sums = ctx.enter_context(nc.psum_tensor("sums", [P, SUM_SLOTS, 512], F32))
        proj = ctx.enter_context(nc.psum_tensor("proj", [P, HALVES, 512], F32))
        turned = ctx.enter_context(nc.psum_tensor("turned", [P, 2, 512], F32))

        src_in, dst_in, rel_in = sem("src_in"), sem("dst_in"), sem("rel_in")
        weight_in, affine_in, x_in = sem("weight_in"), sem("affine_in"), sem("x_in")
        padded = sem("padded")
        consts = sem("consts")
        ones_ready = sem("ones_ready")
        vec = sem("vec")
        src_floats = sem("src_floats")
        src_turned = sem("src_turned")
        source_ready = sem("source_ready")
        keys_rows_ready = sem("keys_rows_ready")
        broken_ready = sem("broken_ready")
        keys_turned = sem("keys_turned")
        flag_ready = sem("flag_ready")
        half_started = sem("half_started")
        stage_loaded = [sem(f"stage_loaded{h}") for h in range(2)]
        gathered = [sem(f"gathered{k}") for k in range(PHASE)]
        selected = sem("selected")
        multiplied = sem("multiplied")
        window_added = sem("window_added")
        margin_folded = sem("margin_folded")
        margin_added = sem("margin_added")
        projected = sem("projected")
        agg_copied = sem("agg_copied")
        tile_cleared = sem("tile_cleared")
        g_staged, g_gathered = sem("g_staged"), sem("g_gathered")
        g_selected, g_multiplied = sem("g_selected"), sem("g_multiplied")
        g_key, g_copied = sem("g_key"), sem("g_copied")
        g_turned, g_shift = sem("g_turned"), sem("g_shift")
        g_projected, g_agg = sem("g_projected"), sem("g_agg")
        tail = sem("tail")
        bn_sd_ready, bn_ready = sem("bn_sd_ready"), sem("bn_ready")
        affined = sem("affined")
        row_ready = sem("row_ready")
        z_ready, z_stats = sem("z_ready"), sem("z_stats")
        ln_ready, ln_sd_ready, ln_rs_ready = sem("ln_ready"), sem("ln_sd_ready"), sem("ln_rs_ready")
        ln_shift_ready = sem("ln_shift_ready")
        pool_normed, act_normed = sem("pool_normed"), sem("act_normed")
        stored = sem("stored")

        block_edges = FULL_BLOCKS * P * P
        last_full = REST_CHUNKS - 1

        def full_blocks(v):
            return v[0:block_edges].rearrange("(q c e) -> c q e", q=FULL_BLOCKS, c=P)

        def rest_block(v):
            return v[block_edges:block_edges + last_full * P].rearrange("(c e) -> c e", e=P)

        def last_chunk(v):
            return v[EDGES - LAST_EDGES:EDGES].rearrange("(c e) -> c e", c=1)

        def load_rows(eng, to, v, done):
            eng.dma_start(to[:, 0:FULL_BLOCKS, :], full_blocks(v)).then_inc(done, 16)
            eng.dma_start(to[0:last_full, FULL_BLOCKS, :], rest_block(v)).then_inc(done, 16)
            eng.dma_start(to[last_full:REST_CHUNKS, FULL_BLOCKS, 0:LAST_EDGES],
                          last_chunk(v)).then_inc(done, 16)

        block = ctx.enter_context(nc.Block())

        @block.sync
        def _(sp):
            sp.wait_ge(padded, 1)
            load_rows(sp, dst_rows, dst, dst_in)
            sp.dma_start(dst_rows[last_full:REST_CHUNKS, FULL_BLOCKS, LAST_EDGES:P],
                         dst[EDGES - (P - LAST_EDGES):EDGES].rearrange("(a b) -> a b", a=1)).then_inc(dst_in, 16)
            load_rows(sp, rel_rows, rel, rel_in)
            sp.dma_start(w_sb[:, :, :, :], weight.rearrange("r (h p) o -> p r h o", p=P)).then_inc(weight_in, 16)
            with nc.allow_non_contiguous_dma(reason="256 values each"):
                sp.dma_start(gamma_t[:, :], gamma.rearrange("(h p) -> p h", p=P)).then_inc(affine_in, 16)
                sp.dma_start(beta_t[:, :], beta.rearrange("(h p) -> p h", p=P)).then_inc(affine_in, 16)
            full = (TILES - 1) * P
            sp.wait_ge(padded, 2)
            sp.dma_start(z[:, 0:TILES - 1, :], x[0:full, :].rearrange("(t p) f -> p t f", p=P)).then_inc(x_in, 16)
            sp.dma_start(z[0:LAST_NODES, TILES - 1, :], x[full:NODES, :]).then_inc(x_in, 16)
            with sp.Fori(0, GROUPS - 1) as g:
                sp.wait_ge(pool_normed, g * 3 + 3)
                sp.wait_ge(act_normed, g * 2 + 2)
                sp.dma_start(out[bass.ds(g * (GROUP * P), GROUP * P), :].rearrange("(t p) f -> p t f", p=P),
                             z[:, bass.ds(g * GROUP, GROUP), :]).then_inc(stored, 16)
            sp.wait_ge(pool_normed, GROUPS * 3)
            sp.wait_ge(act_normed, GROUPS * 2)
            first = (GROUPS - 1) * GROUP
            sp.dma_start(out[first * P:full, :].rearrange("(t p) f -> p t f", p=P),
                         z[:, first:TILES - 1, :]).then_inc(stored, 16)
            sp.dma_start(out[full:NODES, :], z[0:LAST_NODES, TILES - 1, :]).then_inc(stored, 16)
            sp.wait_ge(stored, 16 * (GROUPS + 1))

        @block.gpsimd
        def _(pool):
            pool.memset(ident[:, :], 0.0).then_inc(consts, 1)
            pool.wait_ge(consts, 1)
            pool.affine_select(out=ident[:, :], in_=ident[:, :], compare_op=ALU.not_equal, fill=1.0,
                               base=0, pattern=[[-1, P]], channel_multiplier=1).then_inc(consts, 1)
            pool.iota(lattice[:, :, :], pattern=[[REL_STRIDE, RELS], [1, WINDOW]], base=0, channel_multiplier=0,
                      allow_small_or_imprecise_dtypes=True).then_inc(consts, 1)
            pool.iota(chunk_no[:, 0, :], pattern=[[P, BLOCKS]], base=0, channel_multiplier=1).then_inc(consts, 1)
            pool.iota(lattice_tile[:, :, :], pattern=[[REL_STRIDE, RELS], [1, P]], base=0, channel_multiplier=0,
                      allow_small_or_imprecise_dtypes=True).then_inc(consts, 1)

            def gather(slot, indices, done):
                pool.indirect_dma_start(
                    out=rows[:, slot, :], out_offset=None, in_=x[:, :],
                    in_offset=bass.IndirectOffsetOnAxis(ap=indices, axis=0)).then_inc(done, 16)

            pool.wait_ge(flag_ready, 1)
            bad = pool.value_load(violations[0:1, 0:1], min_val=0, max_val=1)
            with pool.If(bad < 1):
                with pool.Fori(0, PHASES) as i:
                    for h in range(2):
                        pool.wait_ge(stage_loaded[h], i + 1)
                        pool.sem_inc(half_started, 1)
                        for k in range(HALF):
                            gather(h * HALF + k, staged[:, h, k:k + 1], gathered[h * HALF + k])
                pool.wait_ge(stage_loaded[0], PHASES + 1)
                for k in range(REST):
                    gather(k, staged[:, 0, k:k + 1], gathered[k])
            with pool.Else():
                with pool.Fori(0, TILES * CHUNKS) as n:
                    pool.wait_ge(g_staged, n + 1)
                    pool.sem_inc(half_started, 1)
                    gather(0, staged[:, 0, 0:1], g_gathered)

            for g in range(GROUPS):
                pool.wait_ge(ln_rs_ready, g + 1)
                for t in range(g * GROUP, (g + 1) * GROUP, 2):
                    pool.tensor_scalar(z[:, t, :], z[:, t, :], ln[:, t, 0:1], ln_rs[:, t:t + 1],
                                       ALU.subtract, ALU.mult).then_inc(pool_normed, 1)

        @block.scalar
        def _(act):
            act.wait_ge(padded, 1)
            load_rows(act, src_rows, src, src_in)
            act.wait_ge(src_in, 48)
            act.activation(src_f[:, :, :], src_rows[:, :, :], ACT.Copy).then_inc(src_floats, 1)
            act.wait_ge(src_turned, 1)
            act.activation(source[:, 0:CHUNKS], turned[:, 0, 0:CHUNKS], ACT.Copy).then_inc(source_ready, 1)
            act.wait_ge(source_ready, 2)
            act.wait_ge(flag_ready, 1)
            bad = act.value_load(violations[0:1, 0:1], min_val=0, max_val=1)

            def stage(h, column):
                act.activation(staged[:, h, :], source[:, bass.ds(column, HALF)], ACT.Copy).then_inc(stage_loaded[h], 1)

            def copy_agg(column, count, done):
                act.activation(agg_t[:, :, bass.ds(column, count)], proj[:, :, 0:count], ACT.Copy).then_inc(done, 1)

            with act.If(bad < 1):
                stage(0, 0)
                stage(1, HALF)
                with act.Fori(0, PHASES) as i:
                    for h in range(2):
                        act.wait_ge(multiplied, (i + 1) * PHASE + (h + 1) * HALF)
                        stage(h, (i + 1) * PHASE + h * HALF)
                    act.wait_ge(projected, i + 1)
                    copy_agg((i + PAD_TILES - 1) * P, P, agg_copied)
                    act.activation(ring[:, :, :, bass.ds(((i + RING_TILES - 1) & (RING_TILES - 1)) * P, P)],
                                   zeros[:, None, None, :].to_broadcast([P, HALVES, RELS, P]),
                                   ACT.Copy).then_inc(tile_cleared, 1)
                act.wait_ge(projected, PHASES + 1)
                copy_agg((TILES - 2 + PAD_TILES) * P, P, agg_copied)
                act.wait_ge(projected, PHASES + 2)
                copy_agg((TILES - 1 + PAD_TILES) * P, LAST_NODES, agg_copied)
            with act.Else():
                act.wait_ge(g_turned, 1)
                act.activation(key[:, 0:CHUNKS], turned[:, 1, 0:CHUNKS], ACT.Copy).then_inc(g_key, 1)
                with act.Fori(0, TILES) as t:
                    with act.Fori(0, CHUNKS) as c:
                        act.wait_ge(g_multiplied, t * CHUNKS + c + 1)
                        act.activation(staged[:, 0, 0:1], source[:, bass.ds(c, 1)],
                                       ACT.Copy).then_inc(g_staged, 1)
                    act.wait_ge(g_multiplied, (t + 1) * CHUNKS + 1)
                    for h in range(HALVES):
                        act.activation(ring[:, h, :, 0:P],
                                       sums[:, 2 * h:2 * h + 2, :].rearrange("p b (r n) -> p (b r) n", n=P),
                                       ACT.Copy).then_inc(g_copied, 1)
                    act.wait_ge(g_projected, t + 1)
                    copy_agg((t + PAD_TILES) * P, P, g_agg)

            act.wait_ge(tail, 2)
            act.activation(bn_sd[:, :], bn[:, :, 1], ACT.Sqrt, bias=eps[:, 0:1]).then_inc(bn_sd_ready, 1)
            act.wait_ge(bn_ready, 1)
            with act.Fori(0, GROUPS) as g:
                for h in range(HALVES):
                    part = agg_t[:, h, bass.ds((g * GROUP + PAD_TILES) * P, GROUP * P)]
                    act.activation(part, part, ACT.Identity, bias=bn_shift[:, h:h + 1],
                                   scale=bn_scale[:, h:h + 1]).then_inc(affined, 1)
            with act.Fori(0, GROUPS) as g:
                act.wait_ge(ln_ready, g * GROUP + GROUP)
                act.activation(ln_sd[:, bass.ds(g * GROUP, GROUP)], ln[:, bass.ds(g * GROUP, GROUP), 1],
                               ACT.Sqrt, bias=eps[:, 0:1]).then_inc(ln_sd_ready, 1)
                act.wait_ge(ln_shift_ready, g + 1)
                for k in range(1, GROUP, 2):
                    t = g * GROUP + k
                    act.activation(z[:, bass.ds(t, 1), :], z[:, bass.ds(t, 1), :], ACT.Identity,
                                   bias=ln_shift[:, bass.ds(t, 1)],
                                   scale=ln_rs[:, bass.ds(t, 1)]).then_inc(act_normed, 1)

        @block.vector
        def _(dve):
            steps = [0]

            def then(ins):
                steps[0] += 1
                ins.then_inc(vec, 1)
                dve.wait_ge(vec, steps[0])

            then(dve.memset(src_rows[:, FULL_BLOCKS, :], 0))
            then(dve.memset(dst_rows[:, FULL_BLOCKS, :], 0))
            dve.memset(rel_rows[:, FULL_BLOCKS, :], RELS).then_inc(padded, 1)
            dve.memset(ones[:, :], 1.0).then_inc(ones_ready, 1)
            dve.memset(source[:, CHUNKS:TABLE], 0).then_inc(source_ready, 1)
            then(dve.memset(broken[:, :, :], 0.0))
            then(dve.memset(zeros[:, :], 0.0))
            then(dve.memset(eps[:, :], EPS))

            dve.wait_ge(dst_in, 64)
            then(dve.tensor_copy(base[:, :], dst_rows[:, :, 0]))
            for q in range(BLOCKS):
                then(dve.tensor_scalar(offset[:, q, :], dst_rows[:, q, :], base[:, q:q + 1], None, ALU.subtract))
            then(dve.tensor_reduce(extremes[:, 0, :], offset[:, :, :], AX.X, ALU.max))
            then(dve.tensor_reduce(extremes[:, 1, :], offset[:, :, :], AX.X, ALU.min))
            dve.wait_ge(consts, 5)
            then(dve.tensor_scalar(chunk_no[:, 1, :], chunk_no[:, 0, :], float(-PROJECT_AT), None, ALU.add))
            then(dve.tensor_scalar(chunk_no[:, 2, :], chunk_no[:, 1, :], 4, 7,
                                   ALU.arith_shift_right, ALU.logical_shift_left))
            then(dve.tensor_scalar(bounds[:, 1, :], chunk_no[:, 0, :],
                                   float(PHASES * PHASE + REST_PROJECT_AT), float((TILES - 1) * P),
                                   ALU.is_ge, ALU.mult))
            then(dve.tensor_tensor(bounds[:, 0, :], bounds[:, 1, :], chunk_no[:, 2, :], ALU.max))
            then(dve.tensor_scalar(chunk_no[:, 3, :], chunk_no[:, 0, :], 4, 7,
                                   ALU.arith_shift_right, ALU.logical_shift_left))
            then(dve.tensor_scalar(bounds[:, 1, :], chunk_no[:, 3, :], float((RING_TILES - 1) * P - WINDOW),
                                   None, ALU.add))
            for q, n in [(slice(0, FULL_BLOCKS), P), (slice(FULL_BLOCKS, BLOCKS), REST_CHUNKS)]:
                then(dve.tensor_scalar(broken[0:n, 0, q], extremes[0:n, 0, q], float(WINDOW - 1), None, ALU.is_gt))
                then(dve.tensor_scalar(broken[0:n, 1, q], extremes[0:n, 1, q], 0.0, None, ALU.is_lt))
                then(dve.tensor_tensor(broken[0:n, 2, q], base[0:n, q], bounds[0:n, 0, q], ALU.is_lt))
                then(dve.tensor_tensor(broken[0:n, 3, q], base[0:n, q], bounds[0:n, 1, q], ALU.is_gt))
            broken_done = steps[0]
            dve.sem_inc(broken_ready, 1)
            dve.wait_ge(rel_in, 48)
            then(dve.scalar_tensor_tensor(key_rows[:, :, :], rel_rows[:, :, :], float(REL_STRIDE),
                                          offset[:, :, :], ALU.mult, ALU.add))
            dve.sem_inc(keys_rows_ready, 1)
            dve.wait_ge(keys_turned, 1)
            then(dve.tensor_reduce(bounds[0:1, 0, 0:1], proj[0:1, 1, 0:4 * BLOCKS], AX.X, ALU.add))
            then(dve.tensor_scalar(violations[:, :], bounds[0:1, 0, 0:1], 0.0, None, ALU.is_gt))
            then(dve.tensor_copy(place[:, 0:CHUNKS], proj[0:1, 0, 0:CHUNKS]))
            then(dve.tensor_scalar(place[:, 0:CHUNKS], place[:, 0:CHUNKS], RING - 1, None, ALU.bitwise_and))
            then(dve.tensor_copy(key[:, 0:CHUNKS], turned[:, 1, 0:CHUNKS]))
            dve.sem_inc(flag_ready, 1)
            bad = dve.value_load(violations[0:1, 0:1], min_val=0, max_val=1)
            then(dve.memset(agg_t[:, :, :], 0.0))
            dve.memset(z[:, TILES - 1, :], 0.0).then_inc(padded, 1)

            def measure(slot, column, count, done=None):
                for h in range(HALVES):
                    last = dve.bn_stats(stats[:, h, bass.ds(slot, 1), :], agg_t[:, h, bass.ds(column, count)])
                return last

            with dve.If(bad < 1):
                dve.memset(ring[:, :, :, :], 0.0).then_inc(tile_cleared, 1)
                dve.sem_inc(multiplied, PHASE)
                dve.sem_inc(window_added, SUM_SLOTS)
                dve.sem_inc(agg_copied, 1)

                def build_select(c, k):
                    dve.tensor_scalar(select[:, k % SEL_SLOTS, :, :], lattice[:, :, :], key[:, bass.ds(c, 1)],
                                      None, ALU.is_equal).then_inc(selected, 1)

                def add_window(c, k, at):
                    dve.wait_ge(multiplied, c + 1 + PHASE)
                    dve.wait_ge(window_added, c + SUM_SLOTS)
                    dve.tensor_tensor(ring[:, :, :, bass.ds(at, WINDOW)], ring[:, :, :, bass.ds(at, WINDOW)],
                                      sums[:, k % SUM_SLOTS, 0:DIM].rearrange("p (h r n) -> p h r n", h=HALVES, r=RELS),
                                      ALU.add).then_inc(window_added, 1)

                def fold_margin(n, c):
                    dve.wait_ge(window_added, c + SUM_SLOTS)
                    dve.tensor_tensor(ring[:, :, :, 0:WINDOW], ring[:, :, :, 0:WINDOW],
                                      ring[:, :, :, RING:RING + WINDOW], ALU.add).then_inc(margin_added, 1)
                    dve.wait_ge(margin_added, n + 1)
                    dve.memset(ring[:, :, :, RING:RING + WINDOW], 0.0).then_inc(margin_folded, 1)
                    dve.wait_ge(margin_folded, n + 1)

                for c in range(LOOKAHEAD):
                    build_select(c, c)
                dve.wait_ge(tile_cleared, 1)
                with dve.Fori(0, PHASES) as i:
                    _, places = nc.values_load_multi_w_load_instructions(
                        place[0:1, bass.ds(i * PHASE, PHASE)], engines=(mybir.EngineType.DVE,),
                        min_val=0, max_val=RING - 1, skip_runtime_bounds_check_because="masked with RING - 1")
                    dve.wait_ge(tile_cleared, i + 1)
                    for k in range(PHASE):
                        c = i * PHASE + k
                        if k == PROJECT_AT:
                            fold_margin(i, c)
                        if k == 4:
                            dve.wait_ge(agg_copied, i + 1)
                            measure(i, i * P, P)
                        dve.wait_ge(multiplied, c + LOOKAHEAD - SEL_SLOTS + 1 + PHASE)
                        build_select(c + LOOKAHEAD, k + LOOKAHEAD)
                        add_window(c, k, places[k])
                _, places = nc.values_load_multi_w_load_instructions(
                    place[0:1, PHASES * PHASE:CHUNKS], engines=(mybir.EngineType.DVE,),
                    min_val=0, max_val=RING - 1, skip_runtime_bounds_check_because="masked with RING - 1")
                dve.wait_ge(tile_cleared, PHASES + 1)
                for k in range(REST):
                    c = PHASES * PHASE + k
                    if k == REST_PROJECT_AT:
                        fold_margin(PHASES, c)
                    if k == 2:
                        dve.wait_ge(agg_copied, PHASES + 1)
                        measure(PHASES, PHASES * P, P)
                    if k + LOOKAHEAD < REST:
                        dve.wait_ge(multiplied, c + LOOKAHEAD - SEL_SLOTS + 1 + PHASE)
                        build_select(c + LOOKAHEAD, k + LOOKAHEAD)
                    add_window(c, k, places[k])
                fold_margin(PHASES + 1, CHUNKS)
                dve.wait_ge(agg_copied, PHASES + 2)
                measure(PHASES + 1, (PHASES + 1) * P, P)
                dve.wait_ge(agg_copied, PHASES + 3)
                measure(PHASES + 2, (PHASES + 2) * P, LAST_NODES).then_inc(tail, 1)
            with dve.Else():
                for q in range(BLOCKS):
                    dve.tensor_scalar(key_rows[:, q, :], key_rows[:, q, :], base[:, q:q + 1], None,
                                      ALU.add).then_inc(g_shift, 1)
                dve.sem_inc(g_multiplied, 1)
                dve.sem_inc(g_agg, 1)
                dve.wait_ge(g_key, 1)
                with dve.Fori(0, TILES) as t:
                    with dve.Fori(0, CHUNKS) as c:
                        dve.wait_ge(g_multiplied, t * CHUNKS + c + 1)
                        dve.tensor_scalar(select_tile[:, :, :], lattice_tile[:, :, :], key[:, bass.ds(c, 1)],
                                          None, ALU.is_equal).then_inc(g_selected, 1)
                    dve.wait_ge(g_selected, (t + 1) * CHUNKS)
                    dve.tensor_scalar(key[:, 0:CHUNKS], key[:, 0:CHUNKS], float(-P), None,
                                      ALU.add).then_inc(g_shift, 1)
                    dve.wait_ge(g_shift, t + BLOCKS + 1)
                    dve.wait_ge(g_agg, t + 2)
                    measure(t + PAD_TILES, (t + PAD_TILES) * P, P)
                dve.drain()
                measure(TILES - 1 + PAD_TILES, (TILES - 1 + PAD_TILES) * P, LAST_NODES).then_inc(tail, 1)

            done = [1]

            def step(ins):
                done[0] += 1
                ins.then_inc(tail, 1)
                dve.wait_ge(tail, done[0])

            dve.wait_ge(tail, 1)
            dve.bn_aggr(bn[:, 0, :], stats[:, 0, PAD_TILES:, :].rearrange("p t s -> p (t s)"))
            step(dve.bn_aggr(bn[:, 1, :], stats[:, 1, PAD_TILES:, :].rearrange("p t s -> p (t s)")))
            dve.wait_ge(bn_sd_ready, 1)
            step(dve.reciprocal(bn_rs[:, :], bn_sd[:, :]))
            dve.wait_ge(affine_in, 32)
            step(dve.tensor_tensor(bn_scale[:, :], bn_rs[:, :], gamma_t[:, :], ALU.mult))
            step(dve.tensor_tensor(bn_shift[:, :], bn[:, :, 0], bn_scale[:, :], ALU.mult))
            dve.tensor_tensor(bn_shift[:, :], beta_t[:, :], bn_shift[:, :], ALU.subtract).then_inc(bn_ready, 1)
            dve.sem_inc(z_ready, ROW_SLOTS)
            dve.wait_ge(x_in, 32)
            for g in range(GROUPS):
                tiles = range(g * GROUP, (g + 1) * GROUP)
                for t in tiles:
                    dve.wait_ge(row_ready, t + 1)
                    dve.tensor_tensor(z[:, t, :], z[:, t, :], sums[:, t % ROW_SLOTS, 0:DIM],
                                      ALU.add).then_inc(z_ready, 1)
                    if t > tiles[0]:
                        dve.wait_ge(z_ready, t + ROW_SLOTS)
                        dve.bn_stats(ln_stats[:, t - 1, :], z[:, t - 1, :]).then_inc(z_stats, 1)
                dve.wait_ge(z_ready, tiles[-1] + 1 + ROW_SLOTS)
                dve.bn_stats(ln_stats[:, tiles[-1], :], z[:, tiles[-1], :]).then_inc(z_stats, 1)
                dve.wait_ge(z_stats, tiles[-1] + 1)
                for t in tiles:
                    dve.bn_aggr(ln[:, t, :], ln_stats[:, t, :]).then_inc(ln_ready, 1)
                part = slice(g * GROUP, (g + 1) * GROUP)
                dve.wait_ge(ln_sd_ready, g + 1)
                dve.reciprocal(ln_rs[:, part], ln_sd[:, part]).then_inc(ln_rs_ready, 1)
                dve.wait_ge(ln_rs_ready, g + 1)
                dve.scalar_tensor_tensor(ln_shift[:, part], ln[:, part, 0], -1.0, ln_rs[:, part],
                                         ALU.mult, ALU.mult).then_inc(ln_shift_ready, 1)

        @block.tensor
        def _(pe):
            def turn(to, table, q, done=None):
                n = P if q < FULL_BLOCKS else REST_CHUNKS
                return pe.transpose(to[:, q * P:q * P + n], table[0:n, q, :], ident[0:n, 0:n])

            def project(at, count, done):
                for o in range(HALVES):
                    for r in range(RELS):
                        for h in range(HALVES):
                            last = pe.matmul(proj[:, o, 0:count], w_sb[:, r, h, o * P:(o + 1) * P],
                                             ring[:, h, r, bass.ds(at, count)],
                                             start=(r == 0 and h == 0), stop=(r == RELS - 1 and h == HALVES - 1))
                last.then_inc(done, 1)

            pe.wait_ge(consts, 5)
            pe.wait_ge(src_floats, 1)
            for q in range(BLOCKS):
                last = turn(turned[:, 0, :], src_f, q)
            last.then_inc(src_turned, 1)
            pe.wait_ge(broken_ready, 1)
            pe.wait_ge(ones_ready, 1)
            for q in range(BLOCKS):
                n = P if q < FULL_BLOCKS else REST_CHUNKS
                pe.matmul(proj[0:1, 0, q * P:q * P + n], base[0:n, q:q + 1], ident[0:n, 0:n], start=True, stop=True)
            pe.matmul(proj[0:1, 1, 0:4 * BLOCKS], ones[:, 0:1], broken[:, :, :].rearrange("p a q -> p (a q)"),
                      start=True, stop=True)
            pe.wait_ge(keys_rows_ready, 1)
            for q in range(BLOCKS):
                last = turn(turned[:, 1, :], key_rows, q)
            last.then_inc(keys_turned, 1)
            pe.wait_ge(flag_ready, 1)
            bad = pe.value_load(violations[0:1, 0:1], min_val=0, max_val=1)
            pe.wait_ge(weight_in, 16)
            with pe.If(bad < 1):
                def sum_chunk(c, k, phase):
                    pe.wait_ge(gathered[k], (phase + 1) * 16)
                    pe.wait_ge(selected, c + 1)
                    pe.wait_ge(window_added, c + 1)
                    for h in range(HALVES):
                        last = pe.matmul(sums[:, k % SUM_SLOTS, h * P:(h + 1) * P], rows[:, k, h * P:(h + 1) * P],
                                         select[:, k % SEL_SLOTS, :, :].rearrange("p r n -> p (r n)"),
                                         start=True, stop=True)
                    last.then_inc(multiplied, 1)

                pe.wait_ge(tile_cleared, 1)
                with pe.Fori(0, PHASES) as i:
                    for k in range(PHASE):
                        sum_chunk(i * PHASE + k, k, i)
                        if k == PROJECT_AT + 1:
                            pe.wait_ge(margin_folded, i + 1)
                            pe.wait_ge(agg_copied, i + 1)
                            project(((i + RING_TILES - 1) & (RING_TILES - 1)) * P, P, projected)
                for k in range(REST):
                    sum_chunk(PHASES * PHASE + k, k, PHASES)
                    if k == REST_PROJECT_AT + 1:
                        pe.wait_ge(margin_folded, PHASES + 1)
                        pe.wait_ge(agg_copied, PHASES + 1)
                        project((TILES - 2) % RING_TILES * P, P, projected)
                pe.wait_ge(margin_folded, PHASES + 2)
                pe.wait_ge(agg_copied, PHASES + 2)
                project((TILES - 1) % RING_TILES * P, LAST_NODES, projected)
            with pe.Else():
                pe.wait_ge(g_shift, BLOCKS)
                for q in range(BLOCKS):
                    last = turn(turned[:, 1, :], key_rows, q)
                last.then_inc(g_turned, 1)
                with pe.Fori(0, TILES) as t:
                    for b in range(SUM_SLOTS):
                        pe.matmul(sums[:, b, :], zeros[:, :], lattice_tile[:, 0:4, :].rearrange("p r n -> p (r n)"),
                                  start=True, stop=False)
                    with pe.Fori(0, CHUNKS) as c:
                        pe.wait_ge(g_gathered, (t * CHUNKS + c + 1) * 16)
                        pe.wait_ge(g_selected, t * CHUNKS + c + 1)
                        for b in range(SUM_SLOTS):
                            h, part = b // 2, b % 2
                            last = pe.matmul(sums[:, b, :], rows[:, 0, h * P:(h + 1) * P],
                                             select_tile[:, part * 4:part * 4 + 4, :].rearrange("p r n -> p (r n)"),
                                             start=False, stop=False, skip_group_check=True)
                        last.then_inc(g_multiplied, 1)
                    pe.wait_ge(g_copied, (t + 1) * HALVES)
                    pe.wait_ge(g_agg, t + 1)
                    project(0, P, g_projected)

            for t in range(TILES):
                if t % GROUP == 0:
                    pe.wait_ge(affined, (t // GROUP + 1) * HALVES)
                pe.wait_ge(z_ready, t + 1)
                for h in range(HALVES):
                    last = pe.transpose(sums[:, t % ROW_SLOTS, h * P:(h + 1) * P],
                                        agg_t[:, h, (t + PAD_TILES) * P:(t + PAD_TILES + 1) * P], ident[:, :])
                last.then_inc(row_ready, 1)


_INS = ['x', 'src', 'dst', 'edge_type_8', 'L0_gnn_weight', 'L0_gnn_gamma', 'L0_gnn_beta']


def kernel(**inputs):
    import numpy as _np
    import concourse.bacc as _bacc
    from concourse import mybir as _mybir
    from concourse.bass_utils import run_bass_kernel_spmd as _run

    nc = _bacc.Bacc("TRN2", target_bir_lowering=False, num_devices=1)
    arrays, args = {}, []
    for name in _INS:
        a = _np.ascontiguousarray(inputs[name])
        arrays[f"in_{name}"] = a
        args.append(nc.dram_tensor(f"in_{name}", a.shape, _mybir.dt.from_np(a.dtype), kind="ExternalInput").ap())
    result = nc.dram_tensor("out_0", (NODES, DIM), _mybir.dt.float32, kind="ExternalOutput").ap()
    build(nc, *args, result)
    r = _run(nc, [arrays], core_ids=[0])
    return r.results[0]["out_0"]
```

```python
from contextlib import ExitStack

import concourse.bass as bass
from concourse import mybir

F32 = mybir.dt.float32
I32 = mybir.dt.int32
ALU = mybir.AluOpType
ACT = mybir.ActivationFunctionType
AX = mybir.AxisListType

P = 128
NODES, DIM, RELS, EDGES = 3125, 256, 8, 50000
EPS = 1e-5
HALVES = DIM // P
CHUNKS = -(-EDGES // P)
LAST_EDGES = EDGES - (CHUNKS - 1) * P
TILES = -(-NODES // P)
LAST_NODES = NODES - (TILES - 1) * P
WINDOW = P // RELS
PHASE = 16
PHASES = CHUNKS // PHASE
REST = CHUNKS - PHASES * PHASE
PARTS = 4
PART = PHASE // PARTS
PROJECT_AT = PHASE // 2
REST_PROJECT_AT = 4
RING_TILES = 4
RING = RING_TILES * P
REL_STRIDE = 4096
FULL_BLOCKS = CHUNKS // P
REST_CHUNKS = CHUNKS - FULL_BLOCKS * P
BLOCKS = FULL_BLOCKS + 1
TABLE = BLOCKS * P
PAD_TILES = 2
SEL_SLOTS, SUM_SLOTS = 4, 4
LOOKAHEAD = 2
GROUP = 5
GROUPS = TILES // GROUP
ROW_SLOTS = 4


def build(nc, x, src, dst, rel, weight, gamma, beta, out):
    with ExitStack() as ctx:
        def sb(name, shape, dt=F32):
            return ctx.enter_context(nc.sbuf_tensor(name, shape, dt))

        def sem(name):
            return ctx.enter_context(nc.semaphore(name))

        src_rows = sb("src_rows", [P, BLOCKS, P], I32)
        dst_rows = sb("dst_rows", [P, BLOCKS, P], I32)
        rel_rows = sb("rel_rows", [P, BLOCKS, P], I32)
        src_f = sb("src_f", [P, BLOCKS, P])
        base = sb("base", [P, BLOCKS])
        offset = sb("offset", [P, BLOCKS, P])
        key_rows = sb("key_rows", [P, BLOCKS, P])
        extremes = sb("extremes", [P, 2, BLOCKS])
        chunk_no = sb("chunk_no", [P, 4, BLOCKS], I32)
        bounds = sb("bounds", [P, 2, BLOCKS])
        broken = sb("broken", [P, 4, BLOCKS])
        violations = sb("violations", [1, 1], I32)
        source = sb("source", [P, TABLE], I32)
        key = sb("key", [P, TABLE])
        place = sb("place", [1, TABLE], I32)
        staged = sb("staged", [P, PARTS, PART], I32)
        rows = sb("rows", [P, PHASE, DIM])
        lattice = sb("lattice", [P, RELS, WINDOW])
        lattice_tile = sb("lattice_tile", [P, RELS, P])
        select = sb("select", [P, SEL_SLOTS, RELS, WINDOW])
        select_tile = sb("select_tile", [P, RELS, P])
        ident = sb("ident", [P, P])
        ones = sb("ones", [P, P])
        zeros = sb("zeros", [P, P])
        ring = sb("ring", [P, HALVES, RELS, RING + 2 * WINDOW])
        w_sb = sb("w_sb", [P, RELS, HALVES, DIM])
        agg_t = sb("agg_t", [P, HALVES, (PAD_TILES + TILES) * P])
        stats = sb("stats", [P, HALVES, PAD_TILES + TILES, 6])
        bn = sb("bn", [P, HALVES, 2])
        bn_sd = sb("bn_sd", [P, HALVES])
        bn_rs = sb("bn_rs", [P, HALVES])
        bn_scale = sb("bn_scale", [P, HALVES])
        bn_shift = sb("bn_shift", [P, HALVES])
        gamma_t = sb("gamma_t", [P, HALVES])
        beta_t = sb("beta_t", [P, HALVES])
        eps = sb("eps", [P, 1])
        z = sb("z", [P, TILES, DIM])
        ln_stats = sb("ln_stats", [P, TILES, 6])
        ln = sb("ln", [P, TILES, 2])
        ln_sd = sb("ln_sd", [P, TILES])
        ln_rs = sb("ln_rs", [P, TILES])
        ln_shift = sb("ln_shift", [P, TILES])

        sums = ctx.enter_context(nc.psum_tensor("sums", [P, SUM_SLOTS, 512], F32))
        proj = ctx.enter_context(nc.psum_tensor("proj", [P, HALVES, 512], F32))
        turned = ctx.enter_context(nc.psum_tensor("turned", [P, 2, 512], F32))

        src_in, dst_in, rel_in = sem("src_in"), sem("dst_in"), sem("rel_in")
        weight_in, affine_in, x_in = sem("weight_in"), sem("affine_in"), sem("x_in")
        padded = sem("padded")
        consts = sem("consts")
        ones_ready = sem("ones_ready")
        vec = sem("vec")
        src_floats = sem("src_floats")
        src_turned = sem("src_turned")
        source_ready = sem("source_ready")
        key_rows_ready = sem("key_rows_ready")
        broken_counted = sem("broken_counted")
        broken_ready = sem("broken_ready")
        keys_turned = sem("keys_turned")
        flag_ready = sem("flag_ready")
        part_started = sem("part_started")
        stage_loaded = [sem(f"stage_loaded{h}") for h in range(PARTS)]
        gathered = [sem(f"gathered{k}") for k in range(PHASE)]
        selected = sem("selected")
        multiplied = sem("multiplied")
        window_added = sem("window_added")
        margin_folded = sem("margin_folded")
        margin_added = sem("margin_added")
        projected = [sem(f"projected{o}") for o in range(HALVES)]
        agg_copied = [sem(f"agg_copied{o}") for o in range(HALVES)]
        tile_cleared = sem("tile_cleared")
        g_gathered = [sem(f"g_gathered{g}") for g in range(GROUPS)]
        g_staged = sem("g_staged")
        g_selected, g_multiplied = sem("g_selected"), sem("g_multiplied")
        g_summed = sem("g_summed")
        g_key, g_copied = sem("g_key"), sem("g_copied")
        g_turned, g_shift = sem("g_turned"), sem("g_shift")
        g_projected, g_agg = sem("g_projected"), sem("g_agg")
        tail = sem("tail")
        bn_sd_ready, bn_ready = sem("bn_sd_ready"), sem("bn_ready")
        affined = sem("affined")
        row_ready = sem("row_ready")
        z_ready, z_stats = sem("z_ready"), sem("z_stats")
        ln_ready, ln_sd_ready, ln_rs_ready = sem("ln_ready"), sem("ln_sd_ready"), sem("ln_rs_ready")
        ln_shift_ready = sem("ln_shift_ready")
        normed = sem("normed")
        stored = sem("stored")

        block_edges = FULL_BLOCKS * P * P
        last_full = REST_CHUNKS - 1

        def full_blocks(v):
            return v[0:block_edges].rearrange("(q c e) -> c q e", q=FULL_BLOCKS, c=P)

        def rest_block(v):
            return v[block_edges:block_edges + last_full * P].rearrange("(c e) -> c e", e=P)

        def last_chunk(v):
            return v[EDGES - LAST_EDGES:EDGES].rearrange("(c e) -> c e", c=1)

        def load_rows(eng, to, v, done):
            eng.dma_start(to[:, 0:FULL_BLOCKS, :], full_blocks(v)).then_inc(done, 16)
            eng.dma_start(to[0:last_full, FULL_BLOCKS, :], rest_block(v)).then_inc(done, 16)
            eng.dma_start(to[last_full:REST_CHUNKS, FULL_BLOCKS, 0:LAST_EDGES],
                          last_chunk(v)).then_inc(done, 16)

        block = ctx.enter_context(nc.Block())

        @block.sync
        def _(sp):
            sp.wait_ge(padded, 1)
            load_rows(sp, dst_rows, dst, dst_in)
            sp.dma_start(dst_rows[last_full:REST_CHUNKS, FULL_BLOCKS, LAST_EDGES:P],
                         dst[EDGES - (P - LAST_EDGES):EDGES].rearrange("(a b) -> a b", a=1)).then_inc(dst_in, 16)
            load_rows(sp, rel_rows, rel, rel_in)
            sp.dma_start(w_sb[:, :, :, :], weight.rearrange("r (h p) o -> p r h o", p=P)).then_inc(weight_in, 16)
            with nc.allow_non_contiguous_dma(reason="256 values each"):
                sp.dma_start(gamma_t[:, :], gamma.rearrange("(h p) -> p h", p=P)).then_inc(affine_in, 16)
                sp.dma_start(beta_t[:, :], beta.rearrange("(h p) -> p h", p=P)).then_inc(affine_in, 16)
            full = (TILES - 1) * P
            sp.wait_ge(padded, 2)
            sp.dma_start(z[:, 0:TILES - 1, :], x[0:full, :].rearrange("(t p) f -> p t f", p=P)).then_inc(x_in, 16)
            sp.dma_start(z[0:LAST_NODES, TILES - 1, :], x[full:NODES, :]).then_inc(x_in, 16)
            with sp.Fori(0, GROUPS - 1) as g:
                sp.wait_ge(normed, g * GROUP + GROUP)
                sp.dma_start(out[bass.ds(g * (GROUP * P), GROUP * P), :].rearrange("(t p) f -> p t f", p=P),
                             z[:, bass.ds(g * GROUP, GROUP), :]).then_inc(stored, 16)
            sp.wait_ge(normed, TILES)
            first = (GROUPS - 1) * GROUP
            sp.dma_start(out[first * P:full, :].rearrange("(t p) f -> p t f", p=P),
                         z[:, first:TILES - 1, :]).then_inc(stored, 16)
            sp.dma_start(out[full:NODES, :], z[0:LAST_NODES, TILES - 1, :]).then_inc(stored, 16)
            sp.wait_ge(stored, 16 * (GROUPS + 1))

        @block.gpsimd
        def _(pool):
            pool.memset(ident[:, :], 0.0).then_inc(consts, 1)
            pool.wait_ge(consts, 1)
            pool.affine_select(out=ident[:, :], in_=ident[:, :], compare_op=ALU.not_equal, fill=1.0,
                               base=0, pattern=[[-1, P]], channel_multiplier=1).then_inc(consts, 1)
            pool.iota(lattice[:, :, :], pattern=[[REL_STRIDE, RELS], [1, WINDOW]], base=0, channel_multiplier=0,
                      allow_small_or_imprecise_dtypes=True).then_inc(consts, 1)
            pool.iota(chunk_no[:, 0, :], pattern=[[P, BLOCKS]], base=0, channel_multiplier=1).then_inc(consts, 1)
            pool.iota(lattice_tile[:, :, :], pattern=[[REL_STRIDE, RELS], [1, P]], base=0, channel_multiplier=0,
                      allow_small_or_imprecise_dtypes=True).then_inc(consts, 1)

            pool.memset(ring[:, :, :, :], 0.0).then_inc(tile_cleared, 1)

            def gather(slot, indices, done):
                pool.indirect_dma_start(
                    out=rows[:, slot, :], out_offset=None, in_=x[:, :],
                    in_offset=bass.IndirectOffsetOnAxis(ap=indices, axis=0)).then_inc(done, 16)

            pool.wait_ge(flag_ready, 1)
            bad = pool.value_load(violations[0:1, 0:1], min_val=0, max_val=1)
            with pool.If(bad < 1):
                with pool.Fori(0, PHASES) as i:
                    for h in range(PARTS):
                        pool.wait_ge(stage_loaded[h], i + 1)
                        pool.sem_inc(part_started, 1)
                        for k in range(PART):
                            gather(h * PART + k, staged[:, h, k:k + 1], gathered[h * PART + k])
                for k in range(REST):
                    if k % PART == 0:
                        pool.wait_ge(stage_loaded[k // PART], PHASES + 1)
                    gather(k, staged[:, k // PART, k % PART:k % PART + 1], gathered[k])
            with pool.Else():
                for g in range(GROUPS):
                    with pool.Fori(g * GROUP * CHUNKS, (g + 1) * GROUP * CHUNKS) as n:
                        pool.wait_ge(g_staged, n + 1)
                        pool.sem_inc(part_started, 1)
                        gather(0, staged[:, 0, 0:1], g_gathered[g])


        @block.scalar
        def _(act):
            act.wait_ge(padded, 1)
            load_rows(act, src_rows, src, src_in)
            act.wait_ge(src_in, 48)
            act.activation(src_f[:, :, :], src_rows[:, :, :], ACT.Copy).then_inc(src_floats, 1)
            act.wait_ge(src_turned, 1)
            act.activation(source[:, 0:CHUNKS], turned[:, 0, 0:CHUNKS], ACT.Copy).then_inc(source_ready, 1)
            act.wait_ge(source_ready, 2)
            act.wait_ge(flag_ready, 1)
            bad = act.value_load(violations[0:1, 0:1], min_val=0, max_val=1)

            def stage(h, column):
                act.activation(staged[:, h, :], source[:, bass.ds(column, PART)], ACT.Copy).then_inc(stage_loaded[h], 1)

            def copy_agg(o, column, count, done):
                act.activation(agg_t[:, o, bass.ds(column, count)], proj[:, o, 0:count], ACT.Copy).then_inc(done, 1)

            with act.If(bad < 1):
                for h in range(PARTS):
                    stage(h, h * PART)

                def stage_next(i, h):
                    act.wait_ge(multiplied, (i + 1) * PHASE + (h + 1) * PART)
                    stage(h, (i + 1) * PHASE + h * PART)

                with act.Fori(0, PHASES) as i:
                    stage_next(i, 0)
                    stage_next(i, 1)
                    act.wait_ge(projected[1], i + 1)
                    copy_agg(1, i * P, P, agg_copied[1])
                    act.activation(ring[:, :, :, bass.ds(((i + RING_TILES - 2) & (RING_TILES - 1)) * P, P)],
                                   zeros[:, None, None, :].to_broadcast([P, HALVES, RELS, P]),
                                   ACT.Copy).then_inc(tile_cleared, 1)
                    stage_next(i, 2)
                    stage_next(i, 3)
                    act.wait_ge(projected[0], i + 1)
                    copy_agg(0, (i + 1) * P, P, agg_copied[0])
                act.wait_ge(projected[1], PHASES + 1)
                copy_agg(1, PHASES * P, P, agg_copied[1])
                for o in range(HALVES):
                    act.wait_ge(projected[o], PHASES + 1 + o)
                    copy_agg(o, (PHASES + 1) * P, P, agg_copied[o])
                for o in range(HALVES):
                    act.wait_ge(projected[o], PHASES + 2 + o)
                    copy_agg(o, (PHASES + 2) * P, LAST_NODES, agg_copied[o])
            with act.Else():
                act.wait_ge(tile_cleared, 1)
                act.wait_ge(g_turned, 1)
                act.activation(key[:, 0:CHUNKS], turned[:, 1, 0:CHUNKS], ACT.Copy).then_inc(g_key, 1)
                with act.Fori(0, TILES) as t:
                    with act.Fori(0, CHUNKS) as c:
                        act.wait_ge(g_multiplied, t * CHUNKS + c + 1)
                        act.activation(staged[:, 0, 0:1], source[:, bass.ds(c, 1)],
                                       ACT.Copy).then_inc(g_staged, 1)
                    act.wait_ge(g_summed, t + 1)
                    for h in range(HALVES):
                        act.activation(ring[:, h, :, 0:P],
                                       sums[:, 2 * h:2 * h + 2, :].rearrange("p b (r n) -> p (b r) n", n=P),
                                       ACT.Copy).then_inc(g_copied, 1)
                    act.wait_ge(g_projected, (t + 1) * HALVES)
                    for o in range(HALVES):
                        copy_agg(o, (t + PAD_TILES) * P, P, g_agg)

            act.wait_ge(tail, 2)
            act.activation(bn_sd[:, :], bn[:, :, 1], ACT.Sqrt, bias=eps[:, 0:1]).then_inc(bn_sd_ready, 1)
            act.wait_ge(bn_ready, 1)
            with act.Fori(0, GROUPS) as g:
                for h in range(HALVES):
                    part = agg_t[:, h, bass.ds((g * GROUP + PAD_TILES) * P, GROUP * P)]
                    act.activation(part, part, ACT.Identity, bias=bn_shift[:, h:h + 1],
                                   scale=bn_scale[:, h:h + 1]).then_inc(affined, 1)
            with act.Fori(0, GROUPS) as g:
                act.wait_ge(ln_ready, g * GROUP + GROUP)
                act.activation(ln_sd[:, bass.ds(g * GROUP, GROUP)], ln[:, bass.ds(g * GROUP, GROUP), 1],
                               ACT.Sqrt, bias=eps[:, 0:1]).then_inc(ln_sd_ready, 1)
                act.wait_ge(ln_shift_ready, g + 1)
                for k in range(GROUP):
                    t = g * GROUP + k
                    act.activation(z[:, bass.ds(t, 1), :], z[:, bass.ds(t, 1), :], ACT.Identity,
                                   bias=ln_shift[:, bass.ds(t, 1)],
                                   scale=ln_rs[:, bass.ds(t, 1)]).then_inc(normed, 1)

        @block.vector
        def _(dve):
            steps = [0]

            def then(ins):
                steps[0] += 1
                ins.then_inc(vec, 1)
                dve.wait_ge(vec, steps[0])

            then(dve.memset(src_rows[:, FULL_BLOCKS, :], 0))
            then(dve.memset(dst_rows[:, FULL_BLOCKS, :], 0))
            dve.memset(rel_rows[:, FULL_BLOCKS, :], RELS).then_inc(padded, 1)
            dve.memset(ones[:, :], 1.0).then_inc(ones_ready, 1)
            dve.memset(source[:, CHUNKS:TABLE], 0).then_inc(source_ready, 1)
            dve.memset(zeros[:, :], 0.0)
            then(dve.memset(eps[:, :], EPS))

            dve.wait_ge(consts, 4)
            dve.tensor_scalar(chunk_no[:, 1, :], chunk_no[:, 0, :], float(-PROJECT_AT), None, ALU.add)
            dve.tensor_scalar(bounds[:, 1, :], chunk_no[:, 0, :],
                              float(PHASES * PHASE + REST_PROJECT_AT), float((TILES - 1) * P),
                              ALU.is_ge, ALU.mult)
            then(dve.tensor_scalar(chunk_no[:, 3, :], chunk_no[:, 0, :], 4, 7,
                                   ALU.arith_shift_right, ALU.logical_shift_left))
            then(dve.tensor_scalar(chunk_no[:, 2, :], chunk_no[:, 1, :], 4, 7,
                                   ALU.arith_shift_right, ALU.logical_shift_left))
            then(dve.tensor_tensor(bounds[:, 0, :], bounds[:, 1, :], chunk_no[:, 2, :], ALU.max))
            then(dve.tensor_scalar(bounds[:, 1, :], chunk_no[:, 3, :], float((RING_TILES - 2) * P - WINDOW),
                                   None, ALU.add))
            dve.wait_ge(dst_in, 64)
            then(dve.tensor_copy(base[:, :], dst_rows[:, :, 0]))
            then(dve.tensor_tensor(offset[:, :, :], dst_rows[:, :, :],
                                   base[:, :, None].to_broadcast([P, BLOCKS, P]), ALU.subtract))
            dve.wait_ge(rel_in, 48)
            dve.scalar_tensor_tensor(key_rows[:, :, :], rel_rows[:, :, :], float(REL_STRIDE),
                                     offset[:, :, :], ALU.mult, ALU.add).then_inc(key_rows_ready, 1)
            dve.tensor_reduce(extremes[:, 0, :], offset[:, :, :], AX.X, ALU.max)
            then(dve.tensor_reduce(extremes[:, 1, :], offset[:, :, :], AX.X, ALU.min))
            dve.tensor_scalar(broken[:, 0, :], extremes[:, 0, :], float(WINDOW - 1), None, ALU.is_gt)
            dve.tensor_scalar(broken[:, 1, :], extremes[:, 1, :], 0.0, None, ALU.is_lt)
            dve.tensor_tensor(broken[:, 2, :], base[:, :], bounds[:, 0, :], ALU.is_lt)
            dve.tensor_tensor(broken[:, 3, :], base[:, :], bounds[:, 1, :], ALU.is_gt).then_inc(broken_ready, 1)
            dve.wait_ge(keys_turned, 1)
            then(dve.tensor_copy(key[:, 0:CHUNKS], turned[:, 1, 0:CHUNKS]))
            dve.wait_ge(broken_counted, 1)
            then(dve.tensor_reduce(bounds[0:1, 0, 0:1], proj[0:1, 1, 0:4 * BLOCKS], AX.X, ALU.add))
            dve.tensor_scalar(violations[:, :], bounds[0:1, 0, 0:1], 0.0, None, ALU.is_gt).then_inc(flag_ready, 1)
            then(dve.tensor_copy(place[:, 0:CHUNKS], proj[0:1, 0, 0:CHUNKS]))
            then(dve.tensor_scalar(place[:, 0:CHUNKS], place[:, 0:CHUNKS], RING - 1, None, ALU.bitwise_and))
            dve.wait_ge(flag_ready, 1)
            bad = dve.value_load(violations[0:1, 0:1], min_val=0, max_val=1)
            dve.memset(agg_t[:, :, 0:PAD_TILES * P], 0.0)
            then(dve.memset(agg_t[:, :, (TILES - 1 + PAD_TILES) * P:], 0.0))
            dve.memset(z[:, TILES - 1, :], 0.0).then_inc(padded, 1)

            def measure(slot, column, count, done=None):
                for h in range(HALVES):
                    last = dve.bn_stats(stats[:, h, bass.ds(slot, 1), :], agg_t[:, h, bass.ds(column, count)])
                return last

            with dve.If(bad < 1):
                dve.sem_inc(multiplied, PHASE)
                dve.sem_inc(window_added, SUM_SLOTS)
                for o in range(HALVES):
                    dve.sem_inc(agg_copied[o], 1)

                def build_select(c, k):
                    dve.tensor_scalar(select[:, k % SEL_SLOTS, :, :], lattice[:, :, :], key[:, bass.ds(c, 1)],
                                      None, ALU.is_equal).then_inc(selected, 1)

                def add_window(c, k, at):
                    dve.wait_ge(multiplied, c + 1 + PHASE)
                    dve.wait_ge(window_added, c + SUM_SLOTS)
                    dve.tensor_tensor(ring[:, :, :, bass.ds(at, WINDOW)], ring[:, :, :, bass.ds(at, WINDOW)],
                                      sums[:, k % SUM_SLOTS, 0:DIM].rearrange("p (h r n) -> p h r n", h=HALVES, r=RELS),
                                      ALU.add).then_inc(window_added, 1)

                def fold_margin(n, c, idle=0):
                    to = ring[:, :, :, bass.ds(idle * (RING + WINDOW), WINDOW)]
                    of = ring[:, :, :, bass.ds(idle * WINDOW + RING, WINDOW)]
                    dve.wait_ge(window_added, c + SUM_SLOTS)
                    dve.tensor_tensor(to, to, of, ALU.add).then_inc(margin_added, 1)
                    dve.wait_ge(margin_added, n + 1)
                    dve.tensor_scalar(of, zeros[:, None, None, 0:WINDOW].to_broadcast([P, HALVES, RELS, WINDOW]),
                                      0.0, None, ALU.add).then_inc(margin_folded, 1)
                    dve.wait_ge(margin_folded, n + 1)

                for c in range(LOOKAHEAD):
                    build_select(c, c)
                dve.wait_ge(tile_cleared, 1)
                with dve.Fori(0, PHASES) as i:
                    _, places = nc.values_load_multi_w_load_instructions(
                        place[0:1, bass.ds(i * PHASE, PHASE)], engines=(mybir.EngineType.DVE,),
                        min_val=0, max_val=RING - 1, skip_runtime_bounds_check_because="masked with RING - 1")
                    dve.wait_ge(tile_cleared, i + 1)
                    for k in range(PHASE):
                        c = i * PHASE + k
                        if k == PROJECT_AT:
                            away = (i + RING_TILES - 1) & (RING_TILES - 1)
                            fold_margin(i, c, (away + RING_TILES - 1) // RING_TILES)
                        if k == PROJECT_AT + 4:
                            dve.wait_ge(agg_copied[0], i + 1)
                            dve.wait_ge(agg_copied[1], i + 2)
                            measure(i, i * P, P)
                        dve.wait_ge(multiplied, c + LOOKAHEAD - SEL_SLOTS + 1 + PHASE)
                        build_select(c + LOOKAHEAD, k + LOOKAHEAD)
                        add_window(c, k, places[k])
                _, places = nc.values_load_multi_w_load_instructions(
                    place[0:1, PHASES * PHASE:CHUNKS], engines=(mybir.EngineType.DVE,),
                    min_val=0, max_val=RING - 1, skip_runtime_bounds_check_because="masked with RING - 1")
                dve.wait_ge(tile_cleared, PHASES + 1)
                for k in range(REST):
                    c = PHASES * PHASE + k
                    if k == REST_PROJECT_AT:
                        fold_margin(PHASES, c, int((TILES - 2) % RING_TILES > 0))
                    if k + LOOKAHEAD < REST:
                        dve.wait_ge(multiplied, c + LOOKAHEAD - SEL_SLOTS + 1 + PHASE)
                        build_select(c + LOOKAHEAD, k + LOOKAHEAD)
                    add_window(c, k, places[k])
                fold_margin(PHASES + 1, CHUNKS, int((TILES - 1) % RING_TILES > 0))
                for n in range(3):
                    slot = PHASES + n
                    for o in range(HALVES):
                        dve.wait_ge(agg_copied[o], slot + 1 + o)
                    last = measure(slot, slot * P, P if n < 2 else LAST_NODES)
                last.then_inc(tail, 1)
            with dve.Else():
                for q in range(BLOCKS):
                    dve.tensor_scalar(key_rows[:, q, :], key_rows[:, q, :], base[:, q:q + 1], None,
                                      ALU.add).then_inc(g_shift, 1)
                dve.sem_inc(g_multiplied, 1)
                dve.sem_inc(g_agg, HALVES)
                dve.wait_ge(g_key, 1)
                with dve.Fori(0, TILES) as t:
                    with dve.Fori(0, CHUNKS) as c:
                        dve.wait_ge(g_multiplied, t * CHUNKS + c + 1)
                        dve.tensor_scalar(select_tile[:, :, :], lattice_tile[:, :, :], key[:, bass.ds(c, 1)],
                                          None, ALU.is_equal).then_inc(g_selected, 1)
                    dve.wait_ge(g_selected, (t + 1) * CHUNKS)
                    dve.tensor_scalar(key[:, 0:CHUNKS], key[:, 0:CHUNKS], float(-P), None,
                                      ALU.add).then_inc(g_shift, 1)
                    dve.wait_ge(g_shift, t + BLOCKS + 1)
                    dve.wait_ge(g_agg, (t + 2) * HALVES)
                    measure(t + PAD_TILES, (t + PAD_TILES) * P, P)
                dve.drain()
                measure(TILES - 1 + PAD_TILES, (TILES - 1 + PAD_TILES) * P, LAST_NODES).then_inc(tail, 1)

            done = [1]

            def step(ins):
                done[0] += 1
                ins.then_inc(tail, 1)
                dve.wait_ge(tail, done[0])

            dve.wait_ge(tail, 1)
            dve.bn_aggr(bn[:, 0, :], stats[:, 0, PAD_TILES:, :].rearrange("p t s -> p (t s)"))
            step(dve.bn_aggr(bn[:, 1, :], stats[:, 1, PAD_TILES:, :].rearrange("p t s -> p (t s)")))
            dve.wait_ge(bn_sd_ready, 1)
            step(dve.reciprocal(bn_rs[:, :], bn_sd[:, :]))
            dve.wait_ge(affine_in, 32)
            step(dve.tensor_tensor(bn_scale[:, :], bn_rs[:, :], gamma_t[:, :], ALU.mult))
            step(dve.tensor_tensor(bn_shift[:, :], bn[:, :, 0], bn_scale[:, :], ALU.mult))
            dve.tensor_tensor(bn_shift[:, :], beta_t[:, :], bn_shift[:, :], ALU.subtract).then_inc(bn_ready, 1)
            dve.sem_inc(z_ready, ROW_SLOTS)
            dve.wait_ge(x_in, 32)
            for g in range(GROUPS):
                tiles = range(g * GROUP, (g + 1) * GROUP)
                for t in tiles:
                    dve.wait_ge(row_ready, t + 1)
                    dve.tensor_tensor(z[:, t, :], z[:, t, :], sums[:, t % ROW_SLOTS, 0:DIM],
                                      ALU.add).then_inc(z_ready, 1)
                    if t > tiles[0]:
                        dve.wait_ge(z_ready, t + ROW_SLOTS)
                        dve.bn_stats(ln_stats[:, t - 1, :], z[:, t - 1, :]).then_inc(z_stats, 1)
                dve.wait_ge(z_ready, tiles[-1] + 1 + ROW_SLOTS)
                dve.bn_stats(ln_stats[:, tiles[-1], :], z[:, tiles[-1], :]).then_inc(z_stats, 1)
                dve.wait_ge(z_stats, tiles[-1] + 1)
                for t in tiles:
                    dve.bn_aggr(ln[:, t, :], ln_stats[:, t, :]).then_inc(ln_ready, 1)
                part = slice(g * GROUP, (g + 1) * GROUP)
                dve.wait_ge(ln_sd_ready, g + 1)
                dve.reciprocal(ln_rs[:, part], ln_sd[:, part]).then_inc(ln_rs_ready, 1)
                dve.wait_ge(ln_rs_ready, g + 1)
                dve.scalar_tensor_tensor(ln_shift[:, part], ln[:, part, 0], -1.0, ln_rs[:, part],
                                         ALU.mult, ALU.mult).then_inc(ln_shift_ready, 1)

        @block.tensor
        def _(pe):
            def turn(to, table, q, done=None):
                n = P if q < FULL_BLOCKS else REST_CHUNKS
                return pe.transpose(to[:, q * P:q * P + n], table[0:n, q, :], ident[0:n, 0:n])

            def project(o, at, count, first, steps, done):
                for n in range(first, first + steps):
                    r, h = n // HALVES, n % HALVES
                    last = pe.matmul(proj[:, o, 0:count], w_sb[:, r, h, o * P:(o + 1) * P],
                                     ring[:, h, r, bass.ds(at, count)], start=(n == 0), stop=(n == N_STEPS - 1))
                if first + steps == N_STEPS:
                    last.then_inc(done, 1)

            N_STEPS = RELS * HALVES
            PER_STEP = N_STEPS // PROJECT_AT

            pe.wait_ge(consts, 5)
            pe.wait_ge(src_floats, 1)
            for q in range(BLOCKS):
                last = turn(turned[:, 0, :], src_f, q)
            last.then_inc(src_turned, 1)
            pe.wait_ge(key_rows_ready, 1)
            for q in range(BLOCKS):
                last = turn(turned[:, 1, :], key_rows, q)
            last.then_inc(keys_turned, 1)
            pe.wait_ge(broken_ready, 1)
            pe.wait_ge(ones_ready, 1)
            for q in range(BLOCKS):
                n = P if q < FULL_BLOCKS else REST_CHUNKS
                pe.matmul(proj[0:1, 0, q * P:q * P + n], base[0:n, q:q + 1], ident[0:n, 0:n], start=True, stop=True)
                last = pe.matmul(proj[0:1, 1, 4 * q:4 * q + 4], ones[0:n, 0:1], broken[0:n, :, q],
                                 start=True, stop=True)
            last.then_inc(broken_counted, 1)
            pe.wait_ge(flag_ready, 1)
            bad = pe.value_load(violations[0:1, 0:1], min_val=0, max_val=1)
            pe.wait_ge(weight_in, 16)
            with pe.If(bad < 1):
                def sum_chunk(c, k, phase):
                    pe.wait_ge(gathered[k], (phase + 1) * 16)
                    pe.wait_ge(selected, c + 1)
                    pe.wait_ge(window_added, c + 1)
                    for h in range(HALVES):
                        last = pe.matmul(sums[:, k % SUM_SLOTS, h * P:(h + 1) * P], rows[:, k, h * P:(h + 1) * P],
                                         select[:, k % SEL_SLOTS, :, :].rearrange("p r n -> p (r n)"),
                                         start=True, stop=True)
                    last.then_inc(multiplied, 1)

                pe.wait_ge(tile_cleared, 1)
                with pe.Fori(0, PHASES) as i:
                    for k in range(PHASE):
                        sum_chunk(i * PHASE + k, k, i)
                        o, n = int(k >= PROJECT_AT), k % PROJECT_AT * PER_STEP
                        if k == 0:
                            pe.wait_ge(agg_copied[1], i + 1)
                        if k == PROJECT_AT:
                            pe.wait_ge(margin_folded, i + 1)
                            pe.wait_ge(agg_copied[0], i + 1)
                        project(1 - o, ((i + RING_TILES - 2 + o) & (RING_TILES - 1)) * P, P,
                                n, PER_STEP, projected[1 - o])
                at = [(t % RING_TILES) * P for t in (TILES - 3, TILES - 2, TILES - 1)]
                for k in range(REST):
                    sum_chunk(PHASES * PHASE + k, k, PHASES)
                    if k == 0:
                        pe.wait_ge(agg_copied[1], PHASES + 1)
                    if k < REST_PROJECT_AT:
                        project(1, at[0], P, k * N_STEPS // REST_PROJECT_AT, N_STEPS // REST_PROJECT_AT, projected[1])
                    if k == REST_PROJECT_AT:
                        pe.wait_ge(margin_folded, PHASES + 1)
                        pe.wait_ge(agg_copied[0], PHASES + 1)
                    if REST_PROJECT_AT <= k < REST - 1:
                        project(0, at[1], P, (k - REST_PROJECT_AT) * N_STEPS // 2, N_STEPS // 2, projected[0])
                pe.wait_ge(agg_copied[1], PHASES + 2)
                project(1, at[1], P, 0, N_STEPS, projected[1])
                pe.wait_ge(margin_folded, PHASES + 2)
                for o in range(HALVES):
                    pe.wait_ge(agg_copied[o], PHASES + 2 + o)
                    project(o, at[2], LAST_NODES, 0, N_STEPS, projected[o])
            with pe.Else():
                pe.wait_ge(g_shift, BLOCKS)
                for q in range(BLOCKS):
                    last = turn(turned[:, 1, :], key_rows, q)
                last.then_inc(g_turned, 1)
                for g in range(GROUPS):
                    with pe.Fori(g * GROUP, (g + 1) * GROUP) as t:
                        for b in range(SUM_SLOTS):
                            pe.matmul(sums[:, b, :], zeros[:, :], lattice_tile[:, 0:4, :].rearrange("p r n -> p (r n)"),
                                      start=True, stop=False)
                        with pe.Fori(0, CHUNKS) as c:
                            pe.wait_ge(g_gathered[g], ((t - g * GROUP) * CHUNKS + c + 1) * 16)
                            pe.wait_ge(g_selected, t * CHUNKS + c + 1)
                            for b in range(SUM_SLOTS):
                                h, part = b // 2, b % 2
                                last = pe.matmul(sums[:, b, :], rows[:, 0, h * P:(h + 1) * P],
                                                 select_tile[:, part * 4:part * 4 + 4, :].rearrange("p r n -> p (r n)"),
                                                 start=False, stop=False)
                            last.then_inc(g_multiplied, 1)
                        for b in range(SUM_SLOTS):
                            last = pe.matmul(sums[:, b, :], zeros[:, :],
                                             lattice_tile[:, 0:4, :].rearrange("p r n -> p (r n)"),
                                             start=False, stop=True)
                        last.then_inc(g_summed, 1)
                        pe.wait_ge(g_copied, (t + 1) * HALVES)
                        pe.wait_ge(g_agg, (t + 1) * HALVES)
                        for o in range(HALVES):
                            project(o, 0, P, 0, N_STEPS, g_projected)

            for t in range(TILES):
                if t % GROUP == 0:
                    pe.wait_ge(affined, (t // GROUP + 1) * HALVES)
                pe.wait_ge(z_ready, t + 1)
                for h in range(HALVES):
                    last = pe.transpose(sums[:, t % ROW_SLOTS, h * P:(h + 1) * P],
                                        agg_t[:, h, (t + PAD_TILES) * P:(t + PAD_TILES + 1) * P], ident[:, :])
                last.then_inc(row_ready, 1)


_INS = ['x', 'src', 'dst', 'edge_type_8', 'L0_gnn_weight', 'L0_gnn_gamma', 'L0_gnn_beta']


def kernel(**inputs):
    import numpy as _np
    import concourse.bacc as _bacc
    from concourse import mybir as _mybir
    from concourse.bass_utils import run_bass_kernel_spmd as _run

    nc = _bacc.Bacc("TRN2", target_bir_lowering=False, num_devices=1)
    arrays, args = {}, []
    for name in _INS:
        a = _np.ascontiguousarray(inputs[name])
        arrays[f"in_{name}"] = a
        args.append(nc.dram_tensor(f"in_{name}", a.shape, _mybir.dt.from_np(a.dtype), kind="ExternalInput").ap())
    result = nc.dram_tensor("out_0", (NODES, DIM), _mybir.dt.float32, kind="ExternalOutput").ap()
    build(nc, *args, result)
    r = _run(nc, [arrays], core_ids=[0])
    return r.results[0]["out_0"]
```

```python
from contextlib import ExitStack

import concourse.bass as bass
from concourse import mybir

F32 = mybir.dt.float32
I32 = mybir.dt.int32
ALU = mybir.AluOpType
ACT = mybir.ActivationFunctionType
AX = mybir.AxisListType

P = 128
NODES, DIM, RELS, EDGES = 3125, 256, 8, 50000
EPS = 1e-5
HALVES = DIM // P
CHUNKS = -(-EDGES // P)
LAST_EDGES = EDGES - (CHUNKS - 1) * P
TILES = -(-NODES // P)
LAST_NODES = NODES - (TILES - 1) * P
SHIFT = TILES * P - NODES
WINDOW = P // RELS
PHASE = 16
PHASES = CHUNKS // PHASE - 1
REST = CHUNKS - PHASES * PHASE
LAST_AT = 10
PARTS = 4
PART = PHASE // PARTS
STEPS = RELS * DIM // P * (DIM // P)
RING_TILES = 4
RING = RING_TILES * P
REL_STRIDE = 4096
FULL_BLOCKS = CHUNKS // P
REST_CHUNKS = CHUNKS - FULL_BLOCKS * P
BLOCKS = FULL_BLOCKS + 1
TABLE = BLOCKS * P
FOLD_LAG = 2
PAD_TILES = 2
SEL_SLOTS, SUM_SLOTS = 4, 4
LOOKAHEAD = 2
NODE_0 = PAD_TILES * P + SHIFT
BN_STEPS = 4
GROUP = 5
GROUPS = TILES // GROUP
SETS = [(0, 5), (5, 10), (10, 15), (15, 19), (19, 22), (22, TILES)]
ACT_PIECES = [[(0, 4)], [(0, 1), (1, 3), (3, 6), (6, 10), (10, 15)]]
ACT_EARLY = 4
POOL_PIECES = [[(4, 10), (10, 15), (15, 20), (20, TILES)], [(15, 20), (20, TILES)]]
PE_ADDS = (1, 3, 6, 8, 13, 14, 18, 20, 23)
POOL_NORMS, DVE_NORMS = (12, 16, 17, 19, 21), (23, 24)
ROW_SLOTS = 4


def build(nc, x, src, dst, rel, weight, gamma, beta, out):
    with ExitStack() as ctx:
        def sb(name, shape, dt=F32):
            return ctx.enter_context(nc.sbuf_tensor(name, shape, dt))

        def sem(name):
            return ctx.enter_context(nc.semaphore(name))

        src_rows = sb("src_rows", [P, BLOCKS, P], I32)
        dst_rows = sb("dst_rows", [P, BLOCKS, P], I32)
        rel_rows = sb("rel_rows", [P, BLOCKS, P], I32)
        src_f = sb("src_f", [P, BLOCKS, P])
        base = sb("base", [P, BLOCKS])
        offset = sb("offset", [P, BLOCKS, P])
        key_rows = sb("key_rows", [P, BLOCKS, P])
        extremes = sb("extremes", [P, 2, BLOCKS])
        chunk_no = sb("chunk_no", [P, 4, BLOCKS], I32)
        bounds = sb("bounds", [P, 2, BLOCKS])
        broken = sb("broken", [P, 4, BLOCKS])
        violations = sb("violations", [1, 1], I32)
        source = sb("source", [P, TABLE], I32)
        key = sb("key", [P, TABLE])
        place = sb("place", [1, TABLE], I32)
        staged = sb("staged", [P, PARTS, PART], I32)
        rows = sb("rows", [P, PHASE, DIM])
        lattice = sb("lattice", [P, RELS, WINDOW])
        lattice_tile = sb("lattice_tile", [P, RELS, P])
        select = sb("select", [P, SEL_SLOTS, RELS, WINDOW])
        select_tile = sb("select_tile", [P, RELS, P])
        ident = sb("ident", [P, P])
        ones = sb("ones", [P, P])
        zeros = sb("zeros", [P, P])
        ring = sb("ring", [P, HALVES, RELS, RING + 2 * WINDOW])
        w_sb = sb("w_sb", [P, RELS, HALVES, DIM])
        agg_t = sb("agg_t", [P, HALVES, (PAD_TILES + TILES) * P + SHIFT])
        stats = sb("stats", [P, HALVES, PAD_TILES + TILES, 6])
        bn = sb("bn", [P, HALVES, 2])
        bn_sd = sb("bn_sd", [P, HALVES])
        bn_rs = sb("bn_rs", [P, HALVES])
        bn_neg_scale = sb("bn_neg_scale", [P, HALVES])
        bn_scale = sb("bn_scale", [P, HALVES])
        bn_shift = sb("bn_shift", [P, HALVES])
        gamma_t = sb("gamma_t", [P, HALVES])
        beta_t = sb("beta_t", [P, HALVES])
        eps = sb("eps", [P, 1])
        z = sb("z", [P, TILES, DIM])
        ln_stats = sb("ln_stats", [P, TILES, 6])
        ln = sb("ln", [P, TILES, 2])
        ln_sd = sb("ln_sd", [P, TILES])
        ln_rs = sb("ln_rs", [P, TILES])
        ln_shift = sb("ln_shift", [P, TILES])

        sums = ctx.enter_context(nc.psum_tensor("sums", [P, SUM_SLOTS, 512], F32))
        proj = ctx.enter_context(nc.psum_tensor("proj", [P, HALVES, 512], F32))
        turned = ctx.enter_context(nc.psum_tensor("turned", [P, 2, 512], F32))

        src_in, dst_in, rel_in = sem("src_in"), sem("dst_in"), sem("rel_in")
        weight_in, affine_in, x_in = sem("weight_in"), sem("affine_in"), sem("x_in")
        padded = sem("padded")
        consts = sem("consts")
        ones_ready, zeros_ready = sem("ones_ready"), sem("zeros_ready")
        vec = sem("vec")
        src_floats = sem("src_floats")
        src_turned = sem("src_turned")
        source_ready = sem("source_ready")
        key_rows_ready = sem("key_rows_ready")
        broken_counted = sem("broken_counted")
        broken_ready = sem("broken_ready")
        keys_turned = sem("keys_turned")
        flag_ready = sem("flag_ready")
        part_started = sem("part_started")
        first_staged = sem("first_staged")
        stage_loaded = [sem(f"stage_loaded{h}") for h in range(PARTS)]
        gathered = [sem(f"gathered{k}") for k in range(PHASE)]
        selected = sem("selected")
        multiplied = sem("multiplied")
        window_added = sem("window_added")
        margin_added, margin_folded = sem("margin_added"), sem("margin_folded")
        projected = [sem(f"projected{o}") for o in range(HALVES)]
        agg_copied = [sem(f"agg_copied{o}") for o in range(HALVES)]
        ring_cleared = sem("ring_cleared")
        tile_cleared = sem("tile_cleared")
        g_gathered = [sem(f"g_gathered{g}") for g in range(GROUPS)]
        g_staged = sem("g_staged")
        g_lattice = sem("g_lattice")
        g_selected, g_multiplied = sem("g_selected"), sem("g_multiplied")
        g_summed = sem("g_summed")
        g_key, g_copied = sem("g_key"), sem("g_copied")
        g_turned, g_shift = sem("g_turned"), sem("g_shift")
        g_projected, g_agg = sem("g_projected"), sem("g_agg")
        tail = sem("tail")
        bn_sd_ready, bn_ready = sem("bn_sd_ready"), sem("bn_ready")
        affined = [sem(f"affined{h}") for h in range(HALVES)]
        pool_affined = [sem(f"pool_affined{h}") for h in range(HALVES)]
        row_ready = sem("row_ready")
        z_ready, z_stats = sem("z_ready"), sem("z_stats")
        ln_ready, ln_sd_ready, ln_rs_ready = sem("ln_ready"), sem("ln_sd_ready"), sem("ln_rs_ready")
        ln_shift_ready = sem("ln_shift_ready")
        normed, pool_normed, dve_normed = sem("normed"), sem("pool_normed"), sem("dve_normed")
        stored = sem("stored")

        block_edges = FULL_BLOCKS * P * P
        last_full = REST_CHUNKS - 1

        def full_blocks(v):
            return v[0:block_edges].rearrange("(q c e) -> c q e", q=FULL_BLOCKS, c=P)

        def rest_block(v):
            return v[block_edges:block_edges + last_full * P].rearrange("(c e) -> c e", e=P)

        def last_chunk(v):
            return v[EDGES - LAST_EDGES:EDGES].rearrange("(c e) -> c e", c=1)

        def load_blocks(eng, to, v, done):
            eng.dma_start(to[:, 0:FULL_BLOCKS, :], full_blocks(v)).then_inc(done, 16)

        def load_rest(eng, to, v, done):
            eng.dma_start(to[0:last_full, FULL_BLOCKS, :], rest_block(v)).then_inc(done, 16)
            eng.dma_start(to[last_full:REST_CHUNKS, FULL_BLOCKS, 0:LAST_EDGES],
                          last_chunk(v)).then_inc(done, 16)

        dve_adds = [t for t in range(TILES) if t not in PE_ADDS]

        def row_slot(t):
            if t in PE_ADDS:
                n = PE_ADDS.index(t) % ROW_SLOTS
                return (proj if n < HALVES else turned)[:, n % HALVES, 0:DIM]
            return sums[:, dve_adds.index(t) % ROW_SLOTS, 0:DIM]

        def bn_step(h, n):
            return h * BN_STEPS + n

        def affine_done(h, t):
            for done, pieces in ((affined[h], ACT_PIECES[h]), (pool_affined[h], POOL_PIECES[h])):
                for n, (first, end) in enumerate(pieces):
                    if first <= t < end:
                        return done, n + 1

        def set_of(t):
            return next(g for g, (first, end) in enumerate(SETS) if t < end)

        act_norms = [t for t in range(TILES) if t not in POOL_NORMS + DVE_NORMS]

        def wait_normed(eng, first, end):
            for done, tiles in ((normed, act_norms), (pool_normed, POOL_NORMS), (dve_normed, DVE_NORMS)):
                if any(first <= t < end for t in tiles):
                    eng.wait_ge(done, sum(t < end for t in tiles))

        block = ctx.enter_context(nc.Block())

        @block.sync
        def _(sp):
            with nc.allow_non_contiguous_dma(reason="512 values"):
                sp.dma_start(staged[:, 0, :], src[0:PART * P].rearrange("(k e) -> e k", e=P)).then_inc(first_staged, 16)
            load_blocks(sp, dst_rows, dst, dst_in)
            load_blocks(sp, rel_rows, rel, rel_in)
            sp.wait_ge(padded, 1)
            load_rest(sp, dst_rows, dst, dst_in)
            sp.dma_start(dst_rows[last_full:REST_CHUNKS, FULL_BLOCKS, LAST_EDGES:P],
                         dst[EDGES - (P - LAST_EDGES):EDGES].rearrange("(a b) -> a b", a=1)).then_inc(dst_in, 16)
            load_rest(sp, rel_rows, rel, rel_in)
            sp.dma_start(w_sb[:, :, :, :], weight.rearrange("r (h p) o -> p r h o", p=P)).then_inc(weight_in, 16)
            with nc.allow_non_contiguous_dma(reason="256 values each"):
                sp.dma_start(gamma_t[:, :], gamma.rearrange("(h p) -> p h", p=P)).then_inc(affine_in, 16)
                sp.dma_start(beta_t[:, :], beta.rearrange("(h p) -> p h", p=P)).then_inc(affine_in, 16)
            full = (TILES - 1) * P
            sp.wait_ge(gathered[PHASE - 1], 16)
            sp.wait_ge(padded, 2)
            sp.dma_start(z[:, 0:TILES - 1, :], x[0:full, :].rearrange("(t p) f -> p t f", p=P)).then_inc(x_in, 16)
            sp.dma_start(z[0:LAST_NODES, TILES - 1, :], x[full:NODES, :]).then_inc(x_in, 16)
            for first, end in SETS:
                rows_end = min(end, TILES - 1)
                wait_normed(sp, first, rows_end)
                sp.dma_start(out[first * P:rows_end * P, :].rearrange("(t p) f -> p t f", p=P),
                             z[:, first:rows_end, :]).then_inc(stored, 16)
            wait_normed(sp, TILES - 1, TILES)
            sp.dma_start(out[full:NODES, :], z[0:LAST_NODES, TILES - 1, :]).then_inc(stored, 16)
            sp.wait_ge(stored, 16 * (len(SETS) + 1))

        @block.gpsimd
        def _(pool):
            pool.memset(ident[:, :], 0.0).then_inc(consts, 1)
            pool.wait_ge(consts, 1)
            pool.affine_select(out=ident[:, :], in_=ident[:, :], compare_op=ALU.not_equal, fill=1.0,
                               base=0, pattern=[[-1, P]], channel_multiplier=1).then_inc(consts, 1)
            pool.iota(lattice[:, :, :], pattern=[[REL_STRIDE, RELS], [1, WINDOW]], base=0, channel_multiplier=0,
                      allow_small_or_imprecise_dtypes=True).then_inc(consts, 1)
            pool.iota(chunk_no[:, 0, :], pattern=[[P, BLOCKS]], base=0, channel_multiplier=1).then_inc(consts, 1)

            def gather(slot, indices, done):
                pool.indirect_dma_start(
                    out=rows[:, slot, :], out_offset=None, in_=x[:, :],
                    in_offset=bass.IndirectOffsetOnAxis(ap=indices, axis=0)).then_inc(done, 16)

            def gather_part(h, n):
                for k in range(n):
                    gather(h * PART + k, staged[:, h, k:k + 1], gathered[h * PART + k])

            pool.wait_ge(first_staged, 16)
            gather_part(0, PART)
            for h in range(1, PARTS):
                pool.wait_ge(stage_loaded[h], 1)
                gather_part(h, PART)
            pool.wait_ge(flag_ready, 1)
            bad = pool.value_load(violations[0:1, 0:1], min_val=0, max_val=1)
            with pool.If(bad < 1):
                with pool.Fori(1, PHASES) as i:
                    for h in range(PARTS):
                        pool.wait_ge(stage_loaded[h], i + 1)
                        pool.sem_inc(part_started, 1)
                        gather_part(h, PART)
                for n in range(-(-REST // PART)):
                    pool.wait_ge(stage_loaded[n % PARTS], PHASES + 1 + n // PARTS)
                    gather_part(n % PARTS, min(PART, REST - n * PART))
            with pool.Else():
                pool.iota(lattice_tile[:, :, :], pattern=[[REL_STRIDE, RELS], [1, P]], base=0, channel_multiplier=0,
                          allow_small_or_imprecise_dtypes=True).then_inc(g_lattice, 1)
                for g in range(GROUPS):
                    with pool.Fori(g * GROUP * CHUNKS, (g + 1) * GROUP * CHUNKS) as n:
                        pool.wait_ge(g_staged, n + 1)
                        pool.sem_inc(part_started, 1)
                        gather(0, staged[:, 0, 0:1], g_gathered[g])

            for h in range(HALVES):
                pool.wait_ge(bn_ready, h + 1)
                for first, end in POOL_PIECES[h]:
                    part = agg_t[:, h, NODE_0 + first * P:NODE_0 + end * P]
                    pool.tensor_scalar(part, part, bn_scale[:, h:h + 1], bn_shift[:, h:h + 1],
                                       ALU.mult, ALU.add).then_inc(pool_affined[h], 1)
            for t in POOL_NORMS:
                pool.wait_ge(ln_shift_ready, 1 + set_of(t))
                pool.tensor_scalar(z[:, t, :], z[:, t, :], ln_rs[:, t:t + 1], ln_shift[:, t:t + 1],
                                   ALU.mult, ALU.add).then_inc(pool_normed, 1)

        @block.scalar
        def _(act):
            load_blocks(act, src_rows, src, src_in)
            act.wait_ge(padded, 1)
            load_rest(act, src_rows, src, src_in)
            act.wait_ge(zeros_ready, 1)
            act.activation(bn_sd[:, 0:1], eps[:, 0:1], ACT.Sqrt)
            act.wait_ge(src_in, 48)
            act.activation(src_f[:, :, :], src_rows[:, :, :], ACT.Copy).then_inc(src_floats, 1)
            act.wait_ge(src_turned, 1)
            act.activation(source[:, 0:CHUNKS], turned[:, 0, 0:CHUNKS], ACT.Copy).then_inc(source_ready, 1)
            act.wait_ge(source_ready, 2)

            def stage(h, column):
                act.activation(staged[:, h, :], source[:, bass.ds(column, PART)], ACT.Copy).then_inc(stage_loaded[h], 1)

            def copy_agg(o, column, count, done):
                act.activation(agg_t[:, o, bass.ds(column, count)], proj[:, o, 0:count], ACT.Copy).then_inc(done, 1)

            act.wait_ge(first_staged, 16)
            act.sem_inc(stage_loaded[0], 1)
            for h in range(1, PARTS):
                stage(h, h * PART)
            act.wait_ge(zeros_ready, 2)
            act.activation(ring[:, :, :, 0:2 * P], zeros[:, None, None, 0:1].to_broadcast([P, HALVES, RELS, 2 * P]),
                           ACT.Copy).then_inc(tile_cleared, 1)
            act.activation(ring[:, 1, :, 2 * P:],
                           zeros[:, None, 0:1].to_broadcast([P, RELS, RING + 2 * WINDOW - 2 * P]),
                           ACT.Copy).then_inc(tile_cleared, 1)
            def affine(h, first, end):
                part = agg_t[:, h, NODE_0 + first * P:NODE_0 + end * P]
                act.activation(part, part, ACT.Identity, bias=bn_shift[:, h:h + 1],
                               scale=bn_scale[:, h:h + 1]).then_inc(affined[h], 1)

            def batch_norm(h):
                act.wait_ge(tail, bn_step(h, 2))
                act.activation(bn_sd[:, h:h + 1], bn[:, h, 1:2], ACT.Sqrt, bias=eps[:, 0:1]).then_inc(bn_sd_ready, 1)
                act.wait_ge(bn_ready, h + 1)
                for piece in ACT_PIECES[h][:ACT_EARLY]:
                    affine(h, *piece)

            act.wait_ge(flag_ready, 1)
            bad = act.value_load(violations[0:1, 0:1], min_val=0, max_val=1)
            with act.If(bad < 1):
                def stage_next(i, h):
                    act.wait_ge(multiplied, (i + 1) * PHASE + (h + 1) * PART)
                    stage(h, (i + 1) * PHASE + h * PART)

                with act.Fori(0, PHASES) as i:
                    for h in range(PARTS):
                        stage_next(i, h)
                        if h == 1:
                            act.wait_ge(projected[0], i + 1)
                            copy_agg(0, (i - 1 + PAD_TILES) * P, P, agg_copied[0])
                    act.wait_ge(projected[1], i + 1)
                    copy_agg(1, (i - 1 + PAD_TILES) * P, P, agg_copied[1])
                    act.activation(ring[:, :, :, bass.ds(((i + RING_TILES - 1) & (RING_TILES - 1)) * P, P)],
                                   zeros[:, None, None, :].to_broadcast([P, HALVES, RELS, P]),
                                   ACT.Copy).then_inc(tile_cleared, 1)
                for n in range(PARTS, -(-REST // PART)):
                    stage_next(PHASES, n % PARTS)
                for i in range(PHASES, TILES + 1):
                    for o in range(HALVES):
                        act.wait_ge(projected[o], i + 1)
                        copy_agg(o, (i - 1 + PAD_TILES) * P, P, agg_copied[o])
                        if (i, o) == (TILES, 0):
                            batch_norm(0)
            with act.Else():
                act.wait_ge(tile_cleared, 2)
                act.wait_ge(ring_cleared, 2)
                for k in range(PHASE):
                    act.wait_ge(gathered[k], 16)
                act.wait_ge(g_turned, 1)
                act.activation(key[:, 0:CHUNKS], turned[:, 1, 0:CHUNKS], ACT.Copy).then_inc(g_key, 1)
                with act.Fori(0, TILES) as t:
                    with act.Fori(0, CHUNKS) as c:
                        act.wait_ge(g_multiplied, t * CHUNKS + c + 1)
                        act.activation(staged[:, 0, 0:1], source[:, bass.ds(c, 1)],
                                       ACT.Copy).then_inc(g_staged, 1)
                    act.wait_ge(g_summed, t + 1)
                    for h in range(HALVES):
                        act.activation(ring[:, h, :, 0:P],
                                       sums[:, 2 * h:2 * h + 2, :].rearrange("p b (r n) -> p (b r) n", n=P),
                                       ACT.Copy).then_inc(g_copied, 1)
                    act.wait_ge(g_projected, (t + 1) * HALVES)
                    for o in range(HALVES):
                        copy_agg(o, (t + PAD_TILES) * P, P, g_agg)

                batch_norm(0)

            batch_norm(1)
            for g, (first, end) in enumerate(SETS):
                act.wait_ge(ln_ready, end)
                act.activation(ln_sd[:, first:end], ln[:, first:end, 1],
                               ACT.Sqrt, bias=eps[:, 0:1]).then_inc(ln_sd_ready, 1)
                for piece in ACT_PIECES[1][ACT_EARLY + g:ACT_EARLY + g + 1]:
                    affine(1, *piece)
                act.wait_ge(ln_shift_ready, g + 1)
                for t in [t for t in range(first, end) if t in act_norms]:
                    act.activation(z[:, t, :], row_slot(t) if t in PE_ADDS else z[:, t, :], ACT.Identity,
                                   bias=ln_shift[:, t:t + 1], scale=ln_rs[:, t:t + 1]).then_inc(normed, 1)

        @block.vector
        def _(dve):
            steps = [0]

            def then(ins):
                steps[0] += 1
                ins.then_inc(vec, 1)
                dve.wait_ge(vec, steps[0])

            dve.memset(eps[:, :], EPS).then_inc(zeros_ready, 1)
            then(dve.memset(src_rows[:, FULL_BLOCKS, :], 0))
            then(dve.memset(dst_rows[:, FULL_BLOCKS, :], 0))
            dve.memset(rel_rows[:, FULL_BLOCKS, :], RELS).then_inc(padded, 1)
            dve.memset(ones[:, :], 1.0).then_inc(ones_ready, 1)
            dve.memset(source[:, CHUNKS:TABLE], 0).then_inc(source_ready, 1)
            dve.memset(zeros[:, :], 0.0).then_inc(zeros_ready, 1)

            dve.wait_ge(consts, 4)
            then(dve.tensor_scalar(chunk_no[:, 1, :], chunk_no[:, 0, :], float(PHASE // 2), None, ALU.add))
            then(dve.tensor_scalar(chunk_no[:, 2:4, :], chunk_no[:, 0:2, :], 4, 7,
                                   ALU.arith_shift_right, ALU.logical_shift_left))
            then(dve.tensor_scalar(bounds[:, 1, :], chunk_no[:, 0, :], float(PHASES * PHASE + LAST_AT),
                                   float((TILES - 1) * P), ALU.is_ge, ALU.mult))
            then(dve.tensor_tensor(bounds[:, 0, :], bounds[:, 1, :], chunk_no[:, 2, :], ALU.max))
            then(dve.tensor_scalar(bounds[:, 0, :], bounds[:, 0, :], float(-SHIFT), None, ALU.add))
            then(dve.tensor_scalar(bounds[:, 1, :], chunk_no[:, 3, :],
                                   float((RING_TILES - 2) * P - WINDOW - SHIFT), None, ALU.add))
            then(dve.memset(z[:, TILES - 1, :], 0.0))
            dve.sem_inc(padded, 1)
            dve.memset(agg_t[:, :, 0:PAD_TILES * P], 0.0)
            then(dve.memset(agg_t[:, :, (TILES + PAD_TILES) * P:], 0.0))
            dve.memset(ring[:, 0, :, 3 * P:], 0.0).then_inc(ring_cleared, 1)
            dve.wait_ge(dst_in, 64)
            then(dve.tensor_copy(base[:, :], dst_rows[:, :, 0]))
            then(dve.tensor_tensor(offset[:, :, :], dst_rows[:, :, :],
                                   base[:, :, None].to_broadcast([P, BLOCKS, P]), ALU.subtract))
            dve.wait_ge(rel_in, 48)
            dve.scalar_tensor_tensor(key_rows[:, :, :], rel_rows[:, :, :], float(REL_STRIDE),
                                     offset[:, :, :], ALU.mult, ALU.add).then_inc(key_rows_ready, 1)
            dve.tensor_reduce(extremes[:, 0, :], offset[:, :, :], AX.X, ALU.max)
            then(dve.tensor_reduce(extremes[:, 1, :], offset[:, :, :], AX.X, ALU.min))
            dve.tensor_scalar(broken[:, 0, :], extremes[:, 0, :], float(WINDOW - 1), None, ALU.is_gt)
            dve.tensor_scalar(broken[:, 1, :], extremes[:, 1, :], 0.0, None, ALU.is_lt)
            dve.tensor_tensor(broken[:, 2, :], base[:, :], bounds[:, 0, :], ALU.is_lt)
            dve.tensor_tensor(broken[:, 3, :], base[:, :], bounds[:, 1, :], ALU.is_gt).then_inc(broken_ready, 1)
            dve.wait_ge(keys_turned, 1)
            then(dve.tensor_copy(key[:, 0:CHUNKS], turned[:, 1, 0:CHUNKS]))
            dve.memset(ring[:, 0, :, 2 * P:3 * P], 0.0).then_inc(ring_cleared, 1)
            dve.wait_ge(broken_counted, 1)
            then(dve.tensor_reduce(bounds[0:1, 0, 0:1], proj[0:1, 1, 0:4 * BLOCKS], AX.X, ALU.add))
            dve.tensor_scalar(violations[:, :], bounds[0:1, 0, 0:1], 0.0, None, ALU.is_gt).then_inc(flag_ready, 1)
            then(dve.tensor_scalar(place[:, 0:CHUNKS], proj[0:1, 0, 0:CHUNKS], float(SHIFT), None, ALU.add))
            then(dve.tensor_scalar(place[:, 0:CHUNKS], place[:, 0:CHUNKS], RING - 1, None, ALU.bitwise_and))
            dve.wait_ge(flag_ready, 1)
            bad = dve.value_load(violations[0:1, 0:1], min_val=0, max_val=1)

            def measure(o, slot, column, count):
                return dve.bn_stats(stats[:, o, bass.ds(slot, 1), :], agg_t[:, o, bass.ds(column, count)])

            def batch_norm(h):
                dve.wait_ge(tail, bn_step(h, 1))
                dve.bn_aggr(bn[:, h, :], stats[:, h, PAD_TILES:, :].rearrange("p t s -> p (t s)")).then_inc(tail, 1)
                dve.wait_ge(bn_sd_ready, h + 1)
                dve.reciprocal(bn_rs[:, h:h + 1], bn_sd[:, h:h + 1]).then_inc(tail, 1)
                dve.wait_ge(tail, bn_step(h, 3))
                dve.wait_ge(affine_in, 32)
                dve.tensor_tensor(bn_scale[:, h:h + 1], bn_rs[:, h:h + 1], gamma_t[:, h:h + 1], ALU.mult)
                dve.scalar_tensor_tensor(bn_neg_scale[:, h:h + 1], bn_rs[:, h:h + 1], -1.0, gamma_t[:, h:h + 1],
                                         ALU.mult, ALU.mult).then_inc(tail, 1)
                dve.wait_ge(tail, bn_step(h, 4))
                dve.tensor_scalar(bn_shift[:, h:h + 1], bn[:, h, 0:1], bn_neg_scale[:, h:h + 1], beta_t[:, h:h + 1],
                                  ALU.mult, ALU.add).then_inc(bn_ready, 1)

            with dve.If(bad < 1):
                dve.sem_inc(multiplied, PHASE)
                dve.sem_inc(window_added, SUM_SLOTS)
                for o in range(HALVES):
                    dve.sem_inc(agg_copied[o], 1)

                def build_select(c, k):
                    dve.tensor_scalar(select[:, k % SEL_SLOTS, :, :], lattice[:, :, :], key[:, bass.ds(c, 1)],
                                      None, ALU.is_equal).then_inc(selected, 1)

                def add_window(c, k, at):
                    dve.wait_ge(multiplied, c + 1 + PHASE)
                    dve.wait_ge(window_added, c + SUM_SLOTS)
                    dve.tensor_tensor(ring[:, :, :, bass.ds(at, WINDOW)], ring[:, :, :, bass.ds(at, WINDOW)],
                                      sums[:, k % SUM_SLOTS, 0:DIM].rearrange("p (h r n) -> p h r n", h=HALVES, r=RELS),
                                      ALU.add).then_inc(window_added, 1)

                def fold_margin(n, c, idle=0):
                    to = ring[:, :, :, bass.ds(idle * (RING + WINDOW), WINDOW)]
                    of = ring[:, :, :, bass.ds(idle * WINDOW + RING, WINDOW)]
                    dve.wait_ge(window_added, c + SUM_SLOTS)
                    dve.tensor_tensor(to, to, of, ALU.add).then_inc(margin_added, 1)
                    dve.wait_ge(margin_added, n + 1)
                    dve.tensor_scalar(of, zeros[:, None, None, 0:WINDOW].to_broadcast([P, HALVES, RELS, WINDOW]),
                                      0.0, None, ALU.add).then_inc(margin_folded, 1)
                    dve.wait_ge(margin_folded, n + 1)

                for c in range(LOOKAHEAD):
                    build_select(c, c)
                dve.wait_ge(tile_cleared, 2)
                dve.wait_ge(ring_cleared, 2)
                with dve.Fori(0, PHASES) as i:
                    _, places = nc.values_load_multi_w_load_instructions(
                        place[0:1, bass.ds(i * PHASE, PHASE)], engines=(mybir.EngineType.DVE,),
                        min_val=0, max_val=RING - 1, skip_runtime_bounds_check_because="masked with RING - 1")
                    away = (i + RING_TILES - 1) & (RING_TILES - 1)
                    fold_margin(i, i * PHASE, (away + RING_TILES - 1) // RING_TILES)
                    for k in range(PHASE):
                        c = i * PHASE + k
                        if k == PHASE // 2:
                            dve.wait_ge(tile_cleared, i + 2)
                        if k == 4:
                            for o in range(HALVES):
                                dve.wait_ge(agg_copied[o], i + 1)
                                measure(o, i, i * P, P)
                        dve.wait_ge(multiplied, c + LOOKAHEAD - SEL_SLOTS + 1 + PHASE)
                        build_select(c + LOOKAHEAD, k + LOOKAHEAD)
                        add_window(c, k, places[k])
                _, places = nc.values_load_multi_w_load_instructions(
                    place[0:1, PHASES * PHASE:CHUNKS], engines=(mybir.EngineType.DVE,),
                    min_val=0, max_val=RING - 1, skip_runtime_bounds_check_because="masked with RING - 1")
                for k in range(REST):
                    c = PHASES * PHASE + k
                    if k == PHASE // 2:
                        dve.wait_ge(tile_cleared, PHASES + 2)
                    if k == 4:
                        for o in range(HALVES):
                            dve.wait_ge(agg_copied[o], PHASES + 1)
                            measure(o, PHASES, PHASES * P, P)
                            measure(o, PAD_TILES, NODE_0, P - SHIFT)
                    if k == PHASE + 2:
                        for o in range(HALVES):
                            dve.wait_ge(agg_copied[o], PHASES + 2)
                            measure(o, PHASES + 1, (PHASES + 1) * P, P)
                    if k + LOOKAHEAD < REST:
                        dve.wait_ge(multiplied, c + LOOKAHEAD - SEL_SLOTS + 1 + PHASE)
                        build_select(c + LOOKAHEAD, k + LOOKAHEAD)
                    add_window(c, k, places[k])
                fold_margin(PHASES, CHUNKS)
                for o in range(HALVES):
                    for slot in (TILES, TILES + 1):
                        dve.wait_ge(agg_copied[o], slot + 1)
                        last = measure(o, slot, slot * P, P)
                    last.then_inc(tail, 1)
                    if o == 0:
                        batch_norm(0)
            with dve.Else():
                for q in range(BLOCKS):
                    dve.tensor_scalar(key_rows[:, q, :], key_rows[:, q, :], base[:, q:q + 1], float(SHIFT),
                                      ALU.add, ALU.add).then_inc(g_shift, 1)
                dve.sem_inc(g_multiplied, 1)
                dve.sem_inc(g_agg, HALVES)
                dve.wait_ge(g_key, 1)
                dve.wait_ge(g_lattice, 1)
                with dve.Fori(0, TILES) as t:
                    with dve.Fori(0, CHUNKS) as c:
                        dve.wait_ge(g_multiplied, t * CHUNKS + c + 1)
                        dve.tensor_scalar(select_tile[:, :, :], lattice_tile[:, :, :], key[:, bass.ds(c, 1)],
                                          None, ALU.is_equal).then_inc(g_selected, 1)
                    dve.wait_ge(g_selected, (t + 1) * CHUNKS)
                    dve.tensor_scalar(key[:, 0:CHUNKS], key[:, 0:CHUNKS], float(-P), None,
                                      ALU.add).then_inc(g_shift, 1)
                    dve.wait_ge(g_shift, t + BLOCKS + 1)
                    dve.wait_ge(g_agg, (t + 2) * HALVES)
                    for o in range(HALVES):
                        measure(o, t + PAD_TILES, (t + PAD_TILES) * P, P)
                dve.drain()
                for o in range(HALVES):
                    measure(o, PAD_TILES, NODE_0, P - SHIFT).then_inc(tail, 1)
                    if o == 0:
                        batch_norm(0)

            batch_norm(1)
            dve.sem_inc(z_ready, ROW_SLOTS)
            dve.wait_ge(x_in, 32)

            def add_row(t):
                dve.wait_ge(row_ready, t + 1)
                if t not in PE_ADDS:
                    dve.tensor_tensor(z[:, t, :], z[:, t, :], row_slot(t), ALU.add).then_inc(z_ready, 1)

            def row_stats(t):
                if t not in PE_ADDS:
                    dve.wait_ge(z_ready, dve_adds.index(t) + 1 + ROW_SLOTS)
                dve.bn_stats(ln_stats[:, t, :], row_slot(t) if t in PE_ADDS else z[:, t, :]).then_inc(z_stats, 1)

            def aggregate(g):
                dve.wait_ge(z_stats, SETS[g][1])
                for t in range(*SETS[g]):
                    dve.bn_aggr(ln[:, t, :], ln_stats[:, t, :]).then_inc(ln_ready, 1)

            def invert(g):
                part = slice(*SETS[g])
                dve.wait_ge(ln_sd_ready, g + 1)
                dve.reciprocal(ln_rs[:, part], ln_sd[:, part]).then_inc(ln_rs_ready, 1)

            def shift(g):
                part = slice(*SETS[g])
                dve.wait_ge(ln_rs_ready, g + 1)
                dve.scalar_tensor_tensor(ln_shift[:, part], ln[:, part, 0], -1.0, ln_rs[:, part],
                                         ALU.mult, ALU.mult).then_inc(ln_shift_ready, 1)

            for g, (first, end) in enumerate(SETS):
                for t in range(first, end):
                    add_row(t)
                    if g and t == first + 1:
                        aggregate(g - 1)
                    if g and t == first + 2:
                        invert(g - 1)
                    if t:
                        row_stats(t - 1)
                    if g and t == first + 2:
                        shift(g - 1)
            row_stats(TILES - 1)
            last = len(SETS) - 1
            aggregate(last)
            invert(last)
            shift(last)
            dve.wait_ge(ln_shift_ready, len(SETS))
            for t in DVE_NORMS:
                dve.tensor_scalar(z[:, t, :], row_slot(t) if t in PE_ADDS else z[:, t, :],
                                  ln_rs[:, t:t + 1], ln_shift[:, t:t + 1], ALU.mult, ALU.add).then_inc(dve_normed, 1)

        @block.tensor
        def _(pe):
            def turn(to, table, q):
                n = P if q < FULL_BLOCKS else REST_CHUNKS
                return pe.transpose(to[:, q * P:q * P + n], table[0:n, q, :], ident[0:n, 0:n])

            def steps_behind(k, first, end):
                a, b = max(k - first, 0), max(k + 1 - first, 0)
                return range(a * STEPS // (end - first), b * STEPS // (end - first))

            def project(at, steps, free, done):
                for n in steps:
                    o, m = n // (STEPS // 2), n % (STEPS // 2)
                    r, h = m // HALVES, m % HALVES
                    if m == 0:
                        pe.wait_ge(*free[o])
                        pe.wait_ge(weight_in, 16)
                    last = pe.matmul(proj[:, o, 0:P], w_sb[:, r, h, o * P:(o + 1) * P],
                                     ring[:, h, r, bass.ds(at, P)], start=(m == 0), stop=(m == STEPS // 2 - 1))
                    if m == STEPS // 2 - 1:
                        last.then_inc(done[o], 1)

            pe.wait_ge(consts, 4)
            pe.wait_ge(src_floats, 1)
            for q in range(BLOCKS):
                last = turn(turned[:, 0, :], src_f, q)
            last.then_inc(src_turned, 1)
            pe.wait_ge(key_rows_ready, 1)
            for q in range(BLOCKS):
                last = turn(turned[:, 1, :], key_rows, q)
            last.then_inc(keys_turned, 1)
            pe.wait_ge(broken_ready, 1)
            pe.wait_ge(ones_ready, 1)
            for q in range(BLOCKS):
                n = P if q < FULL_BLOCKS else REST_CHUNKS
                pe.matmul(proj[0:1, 0, q * P:q * P + n], base[0:n, q:q + 1], ident[0:n, 0:n], start=True, stop=True)
                last = pe.matmul(proj[0:1, 1, 4 * q:4 * q + 4], ones[0:n, 0:1], broken[0:n, :, q],
                                 start=True, stop=True)
            last.then_inc(broken_counted, 1)
            pe.wait_ge(flag_ready, 1)
            bad = pe.value_load(violations[0:1, 0:1], min_val=0, max_val=1)
            with pe.If(bad < 1):
                def sum_chunk(c, k, phase):
                    pe.wait_ge(gathered[k], (phase + 1) * 16)
                    pe.wait_ge(selected, c + 1)
                    pe.wait_ge(window_added, c + 1)
                    for h in range(HALVES):
                        last = pe.matmul(sums[:, k % SUM_SLOTS, h * P:(h + 1) * P], rows[:, k, h * P:(h + 1) * P],
                                         select[:, k % SEL_SLOTS, :, :].rearrange("p r n -> p (r n)"),
                                         start=True, stop=True)
                    last.then_inc(multiplied, 1)

                pe.wait_ge(tile_cleared, 2)
                pe.wait_ge(ring_cleared, 2)
                with pe.Fori(0, PHASES) as i:
                    for k in range(PHASE):
                        sum_chunk(i * PHASE + k, k, i)
                        if k == FOLD_LAG:
                            pe.wait_ge(margin_folded, i + 1)
                        project(((i + RING_TILES - 1) & (RING_TILES - 1)) * P, steps_behind(k, FOLD_LAG, PHASE),
                                [(agg_copied[o], i + 1) for o in range(HALVES)], projected)
                start = LAST_AT + FOLD_LAG
                for k in range(REST):
                    c = PHASES * PHASE + k
                    sum_chunk(c, k % PHASE, PHASES + k // PHASE)
                    if k == FOLD_LAG:
                        pe.wait_ge(window_added, c - FOLD_LAG + SUM_SLOTS)
                    if FOLD_LAG <= k < start:
                        project((TILES - 3) % RING_TILES * P, steps_behind(k, FOLD_LAG, start),
                                [(agg_copied[o], PHASES + 1) for o in range(HALVES)], projected)
                    if k == start:
                        pe.wait_ge(window_added, c - FOLD_LAG + SUM_SLOTS)
                    if k >= start:
                        project((TILES - 2) % RING_TILES * P, steps_behind(k, start, REST),
                                [(agg_copied[o], PHASES + 2) for o in range(HALVES)], projected)
                pe.wait_ge(margin_folded, PHASES + 1)
                project((TILES - 1) % RING_TILES * P, range(STEPS),
                        [(agg_copied[o], PHASES + 3) for o in range(HALVES)], projected)
            with pe.Else():
                pe.wait_ge(g_lattice, 1)
                pe.wait_ge(g_shift, BLOCKS)
                for q in range(BLOCKS):
                    last = turn(turned[:, 1, :], key_rows, q)
                last.then_inc(g_turned, 1)
                for g in range(GROUPS):
                    with pe.Fori(g * GROUP, (g + 1) * GROUP) as t:
                        for b in range(SUM_SLOTS):
                            pe.matmul(sums[:, b, :], zeros[:, :], lattice_tile[:, 0:4, :].rearrange("p r n -> p (r n)"),
                                      start=True, stop=False)
                        with pe.Fori(0, CHUNKS) as c:
                            pe.wait_ge(g_gathered[g], ((t - g * GROUP) * CHUNKS + c + 1) * 16)
                            pe.wait_ge(g_selected, t * CHUNKS + c + 1)
                            for b in range(SUM_SLOTS):
                                h, part = b // 2, b % 2
                                last = pe.matmul(sums[:, b, :], rows[:, 0, h * P:(h + 1) * P],
                                                 select_tile[:, part * 4:part * 4 + 4, :].rearrange("p r n -> p (r n)"),
                                                 start=False, stop=False)
                            last.then_inc(g_multiplied, 1)
                        for b in range(SUM_SLOTS):
                            last = pe.matmul(sums[:, b, :], zeros[:, :],
                                             lattice_tile[:, 0:4, :].rearrange("p r n -> p (r n)"),
                                             start=False, stop=True)
                        last.then_inc(g_summed, 1)
                        pe.wait_ge(g_copied, (t + 1) * HALVES)
                        project(0, range(STEPS), [(g_agg, (t + 1) * HALVES)] * HALVES, [g_projected] * HALVES)

            pe.wait_ge(x_in, 32)
            for t in range(TILES):
                to = row_slot(t)
                if t in PE_ADDS:
                    if PE_ADDS.index(t) >= ROW_SLOTS:
                        before = PE_ADDS[PE_ADDS.index(t) - ROW_SLOTS]
                        wait_normed(pe, before, before + 1)
                    pe.matmul(to, ident[:, :], z[:, t, :], start=True, stop=False)
                else:
                    pe.wait_ge(z_ready, dve_adds.index(t) + 1)
                for h in range(HALVES):
                    pe.wait_ge(*affine_done(h, t))
                    part = agg_t[:, h, NODE_0 + t * P:NODE_0 + (t + 1) * P]
                    if t in PE_ADDS:
                        last = pe.matmul(to[:, h * P:(h + 1) * P], part, ident[:, :], start=False, stop=(h == HALVES - 1))
                    else:
                        last = pe.transpose(to[:, h * P:(h + 1) * P], part, ident[:, :])
                last.then_inc(row_ready, 1)


_INS = ['x', 'src', 'dst', 'edge_type_8', 'L0_gnn_weight', 'L0_gnn_gamma', 'L0_gnn_beta']


def kernel(**inputs):
    import numpy as _np
    import concourse.bacc as _bacc
    from concourse import mybir as _mybir
    from concourse.bass_utils import run_bass_kernel_spmd as _run

    nc = _bacc.Bacc("TRN2", target_bir_lowering=False, num_devices=1)
    arrays, args = {}, []
    for name in _INS:
        a = _np.ascontiguousarray(inputs[name])
        arrays[f"in_{name}"] = a
        args.append(nc.dram_tensor(f"in_{name}", a.shape, _mybir.dt.from_np(a.dtype), kind="ExternalInput").ap())
    result = nc.dram_tensor("out_0", (NODES, DIM), _mybir.dt.float32, kind="ExternalOutput").ap()
    build(nc, *args, result)
    r = _run(nc, [arrays], core_ids=[0])
    return r.results[0]["out_0"]
```
